# Optimizing a Trainium2 kernel written in Bass

```python
import numpy as np
import jax
import jax.numpy as jnp

def _softmax(x, axis=-1):
    return jax.nn.softmax(x, axis=axis)

def _gelu(x):
    return jax.nn.gelu(x, approximate=True)

def _silu(x):
    return jax.nn.silu(x)

def _sigmoid(x):
    return jax.nn.sigmoid(x)

def _layernorm(x, axis=-1, eps=1e-05):
    m = jnp.mean(x, axis=axis, keepdims=True)
    v = jnp.var(x, axis=axis, keepdims=True)
    return (x - m) / jnp.sqrt(v + eps)

def _scatter_add(tgt, idx, src, axis=0):
    return tgt.at[idx].add(src)

def _segment_sum(src, seg, n):
    return jax.ops.segment_sum(src, seg, n)
kernel_name = 'mk_lm_tower_d1_tok_ids256_r4_a6aacb'

def setup_inputs(seed: int=0):
    np.random.seed(seed)
    _w = jnp.asarray

    def _rec_inputs():
        import jax
        import jax.numpy as jnp
        _rk = jax.random.key(seed)
        x = jax.random.randint(jax.random.fold_in(_rk, 1), (4, 2048), 0, 99990, jnp.int32)
        itok_BS_0_99998 = jax.random.randint(jax.random.fold_in(_rk, 21), (4, 2048), 0, 99999, jnp.int32)
        return (x, itok_BS_0_99998)
    x, itok_BS_0_99998 = _rec_inputs()

    def _L0_tok_setup():
        import jax, jax.numpy as jnp
        import numpy as np
        NUM_EMBEDDINGS = 25000
        EMBED_DIM = 64
        BATCH, SEQ = (16, 1024)
        key = jax.random.key(seed)
        k1, k2, k3 = jax.random.split(key, 3)
        input_one = jax.random.randint(k1, (BATCH, SEQ), 0, NUM_EMBEDDINGS, dtype=jnp.int64 if jax.config.jax_enable_x64 else jnp.int32)
        input_two = jax.random.randint(k2, (BATCH, SEQ), 0, NUM_EMBEDDINGS, dtype=input_one.dtype)
        weight = jax.random.normal(k3, (NUM_EMBEDDINGS, EMBED_DIM), dtype=jnp.float32)
        return {'input_one': input_one, 'input_two': input_two, 'weight': weight}
    _L0_tok_all = _L0_tok_setup()
    _L0_tok_in = {k: v for k, v in _L0_tok_all.items() if k in ('weight',)}
    del _L0_tok_all

    def _L0_attn_setup():
        import jax, jax.numpy as jnp
        import numpy as np
        B, N, C, H = (4, 512, 64, 16)
        D = C // H
        key = jax.random.key(seed)
        k1, k2, k3 = jax.random.split(key, 3)
        x = jax.random.normal(k1, (B, N, C), dtype=jnp.float32)
        w_qkv = jax.random.normal(k2, (C, 3 * C), dtype=jnp.float32) * C ** (-0.5)
        b_qkv = jnp.zeros((3 * C,), dtype=jnp.float32)
        w_proj = jax.random.normal(k3, (C, C), dtype=jnp.float32) * C ** (-0.5)
        b_proj = jnp.zeros((C,), dtype=jnp.float32)
        return {'x': x, 'w_qkv': w_qkv, 'b_qkv': b_qkv, 'w_proj': w_proj, 'b_proj': b_proj}
    _L0_attn_all = _L0_attn_setup()
    _L0_attn_in = {k: v for k, v in _L0_attn_all.items() if k in ('w_qkv', 'b_qkv', 'w_proj', 'b_proj')}
    del _L0_attn_all

    def _L0_ffn_setup():
        import jax, jax.numpy as jnp
        import numpy as np
        NUM_EXPERTS = 8
        TOP_K = 2
        B, S, D = (8, 2048, 64)

        def _moe(tokens, router_w, w1, b1, w2, b2):
            N = tokens.shape[0]
            E = router_w.shape[0]
            logits = tokens.astype(jnp.float32) @ router_w.astype(jnp.float32).T
            probs = jax.nn.softmax(logits, axis=-1)
            rw, re = jax.lax.top_k(probs, TOP_K)
            if TOP_K > 1:
                rw = rw / jnp.maximum(rw.sum(-1, keepdims=True), 1e-12)
            rw = rw.astype(tokens.dtype)
            combine = jnp.zeros((N, E), tokens.dtype).at[jnp.arange(N)[:, None], re].set(rw)
            out = tokens
            for e in range(E):
                h = jax.nn.gelu(tokens @ w1[e] + b1[e], approximate=False)
                y = h @ w2[e] + b2[e]
                out = out + combine[:, e:e + 1] * y
            return out
        key = jax.random.key(seed)
        ks = jax.random.split(key, 4)
        scale = 1.0 / np.sqrt(D).astype(np.float32)
        return {'input_embeddings': jax.random.normal(ks[0], (B, S, D), jnp.float32), 'router_w': jax.random.normal(ks[1], (NUM_EXPERTS, D), jnp.float32) * scale, 'w1': jax.random.normal(ks[2], (NUM_EXPERTS, D, D), jnp.float32) * scale, 'b1': jnp.zeros((NUM_EXPERTS, D), jnp.float32), 'w2': jax.random.normal(ks[3], (NUM_EXPERTS, D, D), jnp.float32) * scale, 'b2': jnp.zeros((NUM_EXPERTS, D), jnp.float32)}
    _L0_ffn_all = _L0_ffn_setup()
    _L0_ffn_in = {k: v for k, v in _L0_ffn_all.items() if k in ('router_w', 'w1', 'b1', 'w2', 'b2')}
    del _L0_ffn_all
    return {'x': x, 'itok_BS_0_99998': itok_BS_0_99998, 'L0_tok_weight': _L0_tok_in['weight'], 'L0_attn_w_qkv': _L0_attn_in['w_qkv'], 'L0_attn_b_qkv': _L0_attn_in['b_qkv'], 'L0_attn_w_proj': _L0_attn_in['w_proj'], 'L0_attn_b_proj': _L0_attn_in['b_proj'], 'L0_ffn_router_w': _L0_ffn_in['router_w'], 'L0_ffn_w1': _L0_ffn_in['w1'], 'L0_ffn_b1': _L0_ffn_in['b1'], 'L0_ffn_w2': _L0_ffn_in['w2'], 'L0_ffn_b2': _L0_ffn_in['b2']}

def reference(x, itok_BS_0_99998, L0_tok_weight, L0_attn_w_qkv, L0_attn_b_qkv, L0_attn_w_proj, L0_attn_b_proj, L0_ffn_router_w, L0_ffn_w1, L0_ffn_b1, L0_ffn_w2, L0_ffn_b2):
    import jax
    import jax.numpy as jnp

    def _L0_tok_ref(input_one, input_two, weight):
        import jax, jax.numpy as jnp
        import numpy as np
        NUM_EMBEDDINGS = 25000
        EMBED_DIM = 64
        BATCH, SEQ = (16, 1024)
        e1 = weight[input_one]
        e2 = weight[input_two]
        same = (input_one == input_two)[..., None]
        return jnp.where(same, e1, e1 + e2)

    def _L0_attn_ref(x, w_qkv, b_qkv, w_proj, b_proj):
        import jax, jax.numpy as jnp
        import numpy as np
        B, N, C, H = (4, 512, 64, 16)
        D = C // H
        b, n, c = x.shape
        qkv = x @ w_qkv + b_qkv
        qkv = qkv.reshape(b, n, 3, H, D)
        q = jnp.transpose(qkv[:, :, 0], (0, 2, 1, 3))
        k = jnp.transpose(qkv[:, :, 1], (0, 2, 1, 3))
        v = jnp.transpose(qkv[:, :, 2], (0, 2, 1, 3))
        attn = jnp.einsum('bhqd,bhkd->bhqk', q, k)
        attn = jax.nn.softmax(attn, axis=-1)
        out = jnp.einsum('bhqk,bhkd->bhqd', attn, v)
        out = jnp.transpose(out, (0, 2, 1, 3)).reshape(b, n, c)
        return out @ w_proj + b_proj

    def _L0_ffn_ref(input_embeddings, router_w, w1, b1, w2, b2):
        import jax, jax.numpy as jnp
        import numpy as np
        NUM_EXPERTS = 8
        TOP_K = 2
        B, S, D = (8, 2048, 64)

        def _moe(tokens, router_w, w1, b1, w2, b2):
            N = tokens.shape[0]
            E = router_w.shape[0]
            logits = tokens.astype(jnp.float32) @ router_w.astype(jnp.float32).T
            probs = jax.nn.softmax(logits, axis=-1)
            rw, re = jax.lax.top_k(probs, TOP_K)
            if TOP_K > 1:
                rw = rw / jnp.maximum(rw.sum(-1, keepdims=True), 1e-12)
            rw = rw.astype(tokens.dtype)
            combine = jnp.zeros((N, E), tokens.dtype).at[jnp.arange(N)[:, None], re].set(rw)
            out = tokens
            for e in range(E):
                h = jax.nn.gelu(tokens @ w1[e] + b1[e], approximate=False)
                y = h @ w2[e] + b2[e]
                out = out + combine[:, e:e + 1] * y
            return out
        b, s, d = input_embeddings.shape
        tokens = input_embeddings.reshape(b * s, d)
        return _moe(tokens, router_w, w1, b1, w2, b2).reshape(b, s, d)
    h = _L0_tok_ref(x, itok_BS_0_99998, L0_tok_weight)
    h = h + _L0_attn_ref(_layernorm(h, axis=-1), L0_attn_w_qkv, L0_attn_b_qkv, L0_attn_w_proj, L0_attn_b_proj)
    h = h + _L0_ffn_ref(_layernorm(h, axis=-1), L0_ffn_router_w, L0_ffn_w1, L0_ffn_b1, L0_ffn_w2, L0_ffn_b2)
    return h

_drawn_inputs = setup_inputs


def setup_inputs(seed=0):
    import zlib

    import numpy as np

    out = dict(_drawn_inputs(seed))
    spreads = {'L0_attn_b_qkv': (0.0, 0.1),
     'L0_attn_b_proj': (0.0, 0.1),
     'L0_ffn_b1': (0.0, 0.425),
     'L0_ffn_b2': (0.0, 0.314)}
    factors = {}
    for name, (base, spread) in spreads.items():
        noise = np.random.default_rng([zlib.crc32(name.encode()), seed]).standard_normal(out[name].shape)
        drawn = base * np.exp(spread * noise) if base else spread * noise
        out[name] = jnp.asarray(drawn.astype(out[name].dtype))
    for name, factor in factors.items():
        out[name] = (out[name] * factor).astype(out[name].dtype)
    return out
```

```python
from contextlib import ExitStack

import concourse.bass as bass
from concourse import mybir
from concourse.alu_op_type import AluOpType as ALU

ACT = mybir.ActivationFunctionType
AX = mybir.AxisListType
F32 = mybir.dt.float32
BF16 = mybir.dt.bfloat16
I32 = mybir.dt.int32
U32 = mybir.dt.uint32

P = 128
VOCAB, C = 25000, 64
B, N = 4, 2048
H, D = 16, 4
E, TOP = 8, 2
EPS = 1e-5
LN_SCALE = 1.0 / C

TILES = N // P
QUARTERS = 4
QT = TILES // QUARTERS
BLK = QT * P
GROUPS, HG = 4, 4
STRIP = 32
TERMS = [(0, 0), (0, 1), (0, 2), (1, 0), (1, 1), (2, 0)]
KROWS = D * len(TERMS)
MROWS = 3
BG = B * GROUPS
UNITS = 4
SLOTS = 32
LEAD = 10
PV_LAG = 5
O_EVAC = 3
O_TURN = 8
M_TURN = 26
PBUF = 4
VW = D + 1
RING_PER_BODY = UNITS * (SLOTS + 2)
MAX_STEPS = 3


def ring_events(first, last):
    out = []
    total = UNITS * SLOTS
    for r in range(total + (SLOTS if last else 0)):
        ahead = r + SLOTS + LEAD
        if not (last and ahead >= total):
            out.append((r, "max", ahead // SLOTS, ahead % SLOTS))
        u = r // SLOTS
        if r % SLOTS == O_TURN and not (first and u == 0) and u <= UNITS:
            out.append((r, "turn_o", u - 1, 0))
        if r % SLOTS == M_TURN and not (last and u + 1 >= UNITS):
            out.append((r, "turn_m", u + 1, 0))
    return [(*e, n) for n, e in enumerate(out)]


RING_BEFORE = SLOTS + LEAD + 1


def ring_base(i):
    if isinstance(i, int) and i == 0:
        return RING_BEFORE
    return i * RING_PER_BODY + (RING_BEFORE - 1)


def bodies(eng, emit):
    emit(0, True, False)
    with eng.Fori(1, BG - 1) as i:
        emit(i, False, False)
    emit(BG - 1, False, True)


def batches(eng, emit, count=B):
    emit(0)
    with eng.Fori(1, count) as b:
        emit(b)


def wait(eng, sem, value):
    if not isinstance(value, int) or value > 0:
        eng.wait_ge(sem, value)


def build(nc, x, itok, table, w_qkv, b_qkv, w_proj, b_proj, router_w, w1, b1, w2, b2, out):
    with ExitStack() as ctx:
        def sb(name, shape, dt=F32):
            return ctx.enter_context(nc.sbuf_tensor(name, shape, dt))

        def sem(name):
            return ctx.enter_context(nc.semaphore(name))

        q_rows = nc.dram_tensor("q_rows", (BG, P, N), BF16, kind="Internal").ap()
        k_rows = nc.dram_tensor("k_rows", (BG, P, N), BF16, kind="Internal").ap()

        ps = ctx.enter_context(nc.psum_tensor("ps", [P, 8, 512], F32))
        RING = 0
        SCORE = 4
        OBANK = 7

        ident = sb("ident", [P, P])
        ident16 = sb("ident16", [P, P], BF16)
        ones = sb("ones", [P, 8 * C])
        wqkv = sb("wqkv", [C + 1, 3 * C])
        wproj = sb("wproj", [C + 1, C])
        wroute = sb("wroute", [C, E])
        w1s = sb("w1s", [C + 1, E * C])
        w2s = sb("w2s", [P, E // 2, C])
        b2s = sb("b2s", [E, C])
        pick = sb("pick", [E, E // 2, P])
        order = sb("order", [P, E])

        ids = sb("ids", [P, 2, B * TILES], I32)
        idsf = sb("idsf", [P, 2, B * TILES])
        negf = sb("negf", [P, 2, B * TILES])
        rows = sb("rows", [P, 2, B * TILES], I32)
        differ_i = sb("differ_i", [P, B * TILES], I32)
        differ = sb("differ", [P, B * TILES])
        hid = sb("hid", [P, B * TILES, C])
        second = sb("second", [P, 2 * TILES, C])
        v_all = sb("v_all", [P, BG, TILES, HG * VW])
        attn = sb("attn", [P, BG, TILES, HG * D])

        lsum = sb("lsum", [P, TILES])
        lvar = sb("lvar", [P, TILES])
        lstd = sb("lstd", [P, TILES])
        lrstd = sb("lrstd", [P, TILES])
        xn = sb("xn", [P, TILES, C])
        sq = sb("sq", [P, TILES, C])
        xnT = sb("xnT", [C + 1, QUARTERS, BLK])
        part = sb("part", [P, 2, 3, BLK], BF16)
        rest = sb("rest", [P, 2, BLK])

        k_slot = sb("k_slot", [P, 2, HG, N], BF16)
        v_slot = sb("v_slot", [P, 2, TILES, HG * VW])
        q_slot = sb("q_slot", [P, UNITS, BLK], BF16)
        q_full = sb("q_full", [P, 2, BLK], BF16)
        prob = sb("prob", [P, PBUF, HG, BLK])
        half_max = sb("half_max", [P, 2, QT * HG])
        neg_max = sb("neg_max", [P, QT, HG])
        rest_max = sb("rest_max", [P, QT, HG])
        m_cols = sb("m_cols", [P, QT, P], BF16)
        o_rows = sb("o_rows", [P, BLK])
        recip = sb("recip", [P, QT, HG])

        at_tok = sb("at_tok", [P, 2, QT, C])
        logits = sb("logits", [P, TILES, E])
        top = sb("top", [P, TILES])
        pr = sb("pr", [P, TILES, E])
        gate = sb("gate", [P, TILES, E])
        eq = sb("eq", [P, TILES, E])
        hot = sb("hot", [P, TILES, E])
        gateT = sb("gateT", [E, QUARTERS, BLK])
        act_h = sb("act_h", [P, 2, BLK])
        gated = sb("gated", [P, E // 2, BLK])
        res = sb("res", [P, TILES, C])

        s_passed = sem("waits_passed")
        s_const = sem("const_ready")
        s_ident = sem("ident_ready")
        s_ones = sem("ones_ready")
        s_vones = sem("value_ones_ready")
        s_zero = sem("psum_zeroed")
        s_w = sem("weights_loaded")
        s_ids = sem("ids_loaded")
        s_row = sem("rows_ready")
        s_idstep = sem("id_steps")
        s_gather = [sem(f"gathered_{n}") for n in range(2)]
        s_pool = sem("pool_steps")
        s_emb = sem("embedded")
        s_ln = sem("ln_steps")
        s_rest = sem("rest_ready")
        s_var = sem("var_ready")
        s_std = sem("std_ready")
        s_xn = sem("xn_ready")
        s_xt = sem("xt_filled")
        s_xnT = sem("xnT_ready")
        s_qk = sem("qk_filled")
        s_qkfree = sem("qk_bank_free")
        s_v = sem("v_filled")
        s_vfree = sem("v_bank_free")
        s_hi = sem("hi_ready")
        s_mid = sem("mid_ready")
        s_lo = sem("lo_ready")
        s_store = [sem(f"stored_{n}") for n in range(2)]
        s_kload = [sem(f"k_loaded_{n}") for n in range(2)]
        s_qload = [sem(f"q_loaded_{n}") for n in range(UNITS)]
        s_vload = [sem(f"v_copied_{n}") for n in range(2)]
        s_fill = sem("ring_filled")
        s_read = sem("ring_read")
        s_pmax = sem("max_steps")
        s_neg = sem("neg_max_ready")
        s_mcols = sem("m_cols_ready")
        s_qfull = sem("q_full_ready")
        s_score = sem("scores_filled")
        s_exp = sem("exps_done")
        s_pv = sem("pv_done")
        s_orow = sem("o_rows_ready")
        s_rec = sem("recip_steps")
        s_part = sem("expert_sum_taken")
        s_tok = sem("at_tok_ready")
        s_atT = sem("atT_filled")
        s_atTr = sem("atT_ready")
        s_proj = sem("proj_filled")
        s_h1 = sem("h1_ready")
        s_x2T = sem("x2T_filled")
        s_x2Tr = sem("x2T_ready")
        s_log = sem("logits_filled")
        s_logr = sem("logits_ready")
        s_shift = sem("shifted")
        s_pex = sem("pexp_ready")
        s_gate = sem("gate_ready")
        s_gT = sem("gateT_filled")
        s_up = sem("up_filled")
        s_gelu = sem("gelu_ready")
        s_gb = sem("gate_rows_filled")
        s_gated = sem("gated_ready")
        s_down = sem("down_filled")
        s_res = sem("res_ready")
        s_out = sem("out_stored")
        s_moe = sem("moe_steps")

        block = ctx.enter_context(nc.Block())

        def flat(ap):
            return ap.rearrange("p a b -> p (a b)")

        def stand_alone(eng):
            eng.sem_inc(s_passed, 1)

        def link(eng, s, base):
            n = [0]

            def step(ins):
                n[0] += 1
                ins.then_inc(s, 1)
                eng.wait_ge(s, base + n[0])
            return step, n

        LN_STEPS = 6
        TOP_STEPS = 19

        def layer_norm(dve, src, dst, t, step, s_v_, s_s_, turn, done):
            def wide(a):
                return a.unsqueeze(2).to_broadcast([P, t, C])
            stand_alone(dve)
            step(nc.vector.reduce_sum(lsum[:, 0:t], src, AX.X))
            step(nc.vector.tensor_scalar(lsum[:, 0:t], lsum[:, 0:t], -LN_SCALE, None, ALU.mult))
            step(nc.vector.tensor_tensor(dst, src, wide(lsum[:, 0:t]), ALU.add))
            step(nc.vector.tensor_tensor(sq[:], dst, dst, ALU.mult))
            step(nc.vector.reduce_sum(lvar[:, 0:t], sq[:], AX.X))
            nc.vector.tensor_scalar(lvar[:, 0:t], lvar[:, 0:t], LN_SCALE, EPS, ALU.mult, ALU.add)\
                .then_inc(s_v_, 1)
            dve.wait_ge(s_s_, turn)
            step(nc.vector.reciprocal(lrstd[:, 0:t], lstd[:, 0:t]))
            nc.vector.tensor_tensor(dst, dst, wide(lrstd[:, 0:t]), ALU.mult).then_inc(done, 1)

        @block.sync
        def _(sp):
            for n, src in enumerate((x, itok)):
                sp.dma_start(ids[:, n, :].rearrange("p (b t) -> p b t", b=B),
                             src.rearrange("b (p t) -> p b t", p=P)).then_inc(s_ids, 16)
            sp.dma_start(wqkv[0:C, :], w_qkv).then_inc(s_w, 16)
            sp.dma_start(wqkv[C:C + 1, :], b_qkv.rearrange("(a n) -> a n", a=1)).then_inc(s_w, 16)
            sp.dma_start(wproj[0:C, :], w_proj).then_inc(s_w, 16)
            sp.dma_start(wproj[C:C + 1, :], b_proj.rearrange("(a n) -> a n", a=1)).then_inc(s_w, 16)
            sp.dma_start(wroute[:], router_w.rearrange("e c -> c e"),
                         allow_slow_non_contiguous=True).then_inc(s_w, 16)
            sp.dma_start(w1s[0:C, :].rearrange("i (e o) -> i e o", e=E),
                         w1.rearrange("e i o -> i e o")).then_inc(s_w, 16)
            sp.dma_start(w1s[C:C + 1, :], b1.rearrange("(a e) o -> a (e o)", a=1)).then_inc(s_w, 16)
            sp.dma_start(w2s[:], w2.rearrange("(r e) i o -> (e i) r o", e=2)).then_inc(s_w, 16)
            sp.dma_start(b2s[:], b2).then_inc(s_w, 16)

            def store_rows(b):
                for q in range(QUARTERS):
                    n = q % 2
                    wait(sp, s_hi, b * QUARTERS + q + 1)
                    wait(sp, s_mid, b * QUARTERS + q + 1)
                    wait(sp, s_lo, b * QUARTERS + q + 1)
                    for t, (pq, pk) in enumerate(TERMS):
                        for dst, side, p0 in ((q_rows, pq, 0), (k_rows, pk, C)):
                            d = dst[bass.ds(b * GROUPS, GROUPS), :, q * BLK:(q + 1) * BLK]
                            d = d.rearrange("g (j r) n -> g j r n", r=STRIP)[:, :, D * t:D * t + D, :]
                            sp.dma_start(d, part[p0:p0 + C, n, side, :]).then_inc(s_store[n], 16)
            batches(sp, store_rows)

            for n in range(2):
                sp.wait_ge(s_store[n], 16 * 2 * len(TERMS) * B * 2)
            sp.wait_ge(s_ones, 2 + HG)
            sp.wait_ge(s_zero, 2)

            def load_k(n, i):
                for j in range(HG):
                    lo = STRIP * j
                    sp.dma_start(k_slot[lo:lo + KROWS, n, j, :],
                                 k_rows[bass.ds(i, 1), lo:lo + KROWS, :].rearrange("a r n -> (a r) n"))\
                        .then_inc(s_kload[n], 16)

            def load_q(u, i):
                for j in range(HG):
                    lo = STRIP * j
                    sp.dma_start(q_slot[lo:lo + KROWS, u, :],
                                 k_or_q(q_rows, i, lo, u)).then_inc(s_qload[u], 16)

            def k_or_q(t, i, lo, u):
                return t[bass.ds(i, 1), lo:lo + KROWS, u * BLK:(u + 1) * BLK].rearrange("a r n -> (a r) n")

            load_q(0, 0)
            load_k(0, 0)
            load_q(1, 0)
            load_k(1, 0)
            load_q(2, 0)
            load_q(3, 0)

            def reload(i):
                blocks = 2 * SLOTS
                for u in range(UNITS):
                    sp.wait_ge(s_exp, i * (UNITS * blocks) + (u + 1) * blocks)
                    load_q(u, i + 1)
                    if u == 1:
                        load_k(0, i + 1)
                    if u == 3:
                        load_k(1, i + 1)

            def reload_of(i):
                reload(i)
            batches(sp, reload_of, BG - 1)

            def store_out(b):
                wait(sp, s_res, b + 1)
                sp.dma_start(out[bass.ds(b, 1), :, :].rearrange("a (p t) c -> (a p) (t c)", p=P),
                             res[:].rearrange("p t c -> p (t c)")).then_inc(s_out, 16)
                wait(sp, s_out, b * 16 + 16)
                stand_alone(sp)
            batches(sp, store_out)

        @block.gpsimd
        def _(pool):
            nc.gpsimd.memset(ident[:], 0.0).then_inc(s_ident, 1)
            nc.gpsimd.memset(ident16[:], 0.0).then_inc(s_ident, 1)
            nc.gpsimd.memset(pick[:], 1.0).then_inc(s_ident, 1)
            nc.gpsimd.iota(order[:], [[-1, E]], base=E, channel_multiplier=0,
                           allow_small_or_imprecise_dtypes=True).then_inc(s_ident, 1)
            pool.wait_ge(s_ident, 4)
            for m in (ident, ident16):
                nc.gpsimd.affine_select(out=m[:], in_=m[:], compare_op=ALU.not_equal, fill=1.0, base=0,
                                        pattern=[[-1, P]], channel_multiplier=1).then_inc(s_const, 1)
            nc.gpsimd.affine_select(out=pick[:], in_=pick[:], compare_op=ALU.is_ge, fill=0.0, base=0,
                                    pattern=[[P, E // 2], [1, P]], channel_multiplier=-C).then_inc(s_const, 1)
            pool.wait_ge(s_const, 3)
            nc.gpsimd.affine_select(out=pick[:], in_=pick[:], compare_op=ALU.is_ge, fill=0.0, base=C - 1,
                                    pattern=[[-P, E // 2], [-1, P]], channel_multiplier=C).then_inc(s_const, 1)
            nc.gpsimd.memset(v_all[:], 1.0).then_inc(s_vones, 1)
            nc.gpsimd.memset(m_cols[:], 0.0).then_inc(s_vones, 1)

            pool.wait_ge(s_row, 1)

            def gather(b):
                for t in range(b * TILES, (b + 1) * TILES):
                    for n, dst in enumerate((hid[:, t, :], second[:, t % (2 * TILES), :])):
                        nc.gpsimd.indirect_dma_start(
                            out=dst, out_offset=None, in_=table,
                            in_offset=bass.IndirectOffsetOnAxis(ap=rows[:, n, t:t + 1], axis=0))\
                            .then_inc(s_gather[b % 2], 16)

            gather(0)
            for b in range(B):
                if b + 1 < B:
                    if b >= 1:
                        pool.wait_ge(s_emb, b)
                    gather(b + 1)
                pool.wait_ge(s_gather[b % 2], 16 * 2 * TILES * (b // 2 + 1))
                tiles = slice(b * TILES, (b + 1) * TILES)
                half = slice(b % 2 * TILES, (b % 2 + 1) * TILES)
                nc.gpsimd.tensor_tensor(second[:, half, :], second[:, half, :],
                                        differ[:, tiles].unsqueeze(2).to_broadcast([P, TILES, C]),
                                        ALU.mult).then_inc(s_pool, 1)
                wait(pool, s_pool, b + 1)
                nc.gpsimd.tensor_tensor(hid[:, tiles, :], hid[:, tiles, :], second[:, half, :],
                                        ALU.add).then_inc(s_emb, 1)

            def split_rows(b):
                for q in range(QUARTERS):
                    n = q % 2
                    turn = b * QUARTERS + q + 1
                    wait(pool, s_rest, b * QUARTERS + q + 1)
                    wait(pool, s_store[n], 16 * 2 * len(TERMS) * (b * 2 + q // 2))
                    stand_alone(pool)
                    nc.gpsimd.tensor_copy(part[:, n, 1, :], rest[:, n, :]).then_inc(s_mid, 1)
                    pool.wait_ge(s_mid, turn)
                    nc.gpsimd.tensor_tensor(part[:, n, 2, :], rest[:, n, :], part[:, n, 1, :],
                                            ALU.subtract).then_inc(s_lo, 1)
            batches(pool, split_rows)

            def copy_v(n, i):
                stand_alone(pool)
                nc.gpsimd.tensor_copy(v_slot[:, n, :, :].unsqueeze(1), v_all[:, bass.ds(i, 1), :, :])\
                    .then_inc(s_vload[n], 1)

            def split_max(unit, count):
                index, turned = count
                step, n = link(pool, s_pmax, MAX_STEPS * index)
                pool.wait_ge(s_neg, index + 1)
                cols = m_cols[:, :, :].rearrange("p q (j r) -> p q j r", r=STRIP)
                if turned is not None:
                    pool.wait_ge(s_fill, turned)
                stand_alone(pool)
                step(nc.gpsimd.tensor_copy(cols[:, :, :, KROWS], neg_max[:]))
                step(nc.gpsimd.tensor_tensor(rest_max[:], neg_max[:], cols[:, :, :, KROWS], ALU.subtract))
                stand_alone(pool)
                step(nc.gpsimd.tensor_copy(cols[:, :, :, KROWS + 1], rest_max[:]))
                nc.gpsimd.tensor_tensor(cols[:, :, :, KROWS + 2], rest_max[:], cols[:, :, :, KROWS + 1],
                                        ALU.subtract).then_inc(s_mcols, 1)

            pool.wait_ge(s_vones, 2)
            pool.wait_ge(s_vfree, B * QUARTERS)
            copy_v(0, 0)
            copy_v(1, 0)
            split_max(0, (0, None))

            def body(i, first, last):
                base = ring_base(i)
                turn = {u: n for _, kind, u, _, n in ring_events(first, last) if kind == "turn_m"}
                end = {u: n for _, kind, u, it, n in ring_events(first, last) if kind == "max" and it == SLOTS - 1}
                for u in range(UNITS):
                    if (u + 1) in end:
                        if u in turn:
                            before = base + turn[u] + 1
                        elif first:
                            before = SLOTS + LEAD + 1
                        else:
                            before = base + turn[UNITS] + 1 - RING_PER_BODY if UNITS in turn else \
                                base + {v: n for _, k, v, _, n in ring_events(False, False) if k == "turn_m"}[UNITS] \
                                + 1 - RING_PER_BODY
                        split_max(u + 1, (i * UNITS + u + 1, before))
                    if not last and u == 2:
                        pool.wait_ge(s_pv, i * (UNITS * TILES) + 2 * TILES)
                        copy_v(0, i + 1)
                    if not first and u == 0:
                        pool.wait_ge(s_pv, i * (UNITS * TILES))
                        copy_v(1, i)
            bodies(pool, body)

            def order_tokens(b):
                for q in range(QUARTERS):
                    n = q % 2
                    wait(pool, s_atT, b * QUARTERS + q - 1)
                    stand_alone(pool)
                    nc.gpsimd.tensor_copy(
                        at_tok[:, n, :, :].rearrange("p t (g c) -> p g t c", g=GROUPS),
                        attn[:, bass.ds(b * GROUPS, GROUPS), QT * q:QT * q + QT, :]).then_inc(s_tok, 1)
            batches(pool, order_tokens)

        @block.vector
        def _(dve):
            nc.vector.memset(ps[:], 0.0).then_inc(s_zero, 1)
            nc.vector.memset(xnT[:], 1.0).then_inc(s_ones, 1)
            nc.vector.memset(k_slot[:], 0.0).then_inc(s_ones, 1)
            dve.wait_ge(s_ones, 2)
            for j in range(HG):
                nc.vector.memset(k_slot[STRIP * j:STRIP * j + STRIP, :, j, :], 1.0).then_inc(s_ones, 1)
            nc.vector.memset(q_slot[:], 0.0).then_inc(s_zero, 1)
            dve.wait_ge(s_ids, 32)
            step, _ = link(dve, s_idstep, 0)
            step(nc.vector.tensor_copy(idsf[:], ids[:]))
            step(nc.vector.tensor_scalar(negf[:], idsf[:], 0.0, float(VOCAB), ALU.is_lt, ALU.mult))
            step(nc.vector.tensor_tensor(idsf[:], idsf[:], negf[:], ALU.add))
            step(nc.vector.tensor_scalar(idsf[:], idsf[:], 0.0, float(VOCAB - 1), ALU.max, ALU.min))
            step(nc.vector.tensor_copy(rows[:], idsf[:]))
            step(nc.vector.tensor_tensor(differ_i[:], ids[:, 0, :], ids[:, 1, :], ALU.bitwise_xor))
            nc.vector.tensor_scalar(differ[:], differ_i[:], 0.0, None, ALU.not_equal).then_inc(s_row, 1)

            def normalise(b):
                step, n_ = link(dve, s_ln, b * LN_STEPS)
                wait(dve, s_emb, b + 1)
                wait(dve, s_xt, b * QUARTERS)
                layer_norm(dve, hid[:, bass.ds(b * TILES, TILES), :], xn[:], TILES, step,
                           s_var, s_std, b + 1, s_xn)
                for q in range(QUARTERS):
                    n = q % 2
                    wait(dve, s_hi, b * QUARTERS + q + 1)
                    wait(dve, s_lo, b * QUARTERS + q - 1)
                    nc.vector.tensor_tensor(rest[:, n, :], ps[:, 4 + n, :], part[:, n, 0, :], ALU.subtract)\
                        .then_inc(s_rest, 1)
            batches(dve, normalise)

            def reduce_item(use, unit, item):
                q, j, h = item // 8, (item // 2) % HG, item % 2
                pair = RING + 2 * (use % 2)
                nc.vector.tensor_reduce(half_max[:, h, HG * q + j:HG * q + j + 1],
                                        ps[:, pair:pair + 2, :], AX.XY, ALU.max, negate=True)\
                    .then_inc(s_read, 1)

            def place_max(use, unit, count, u_global):
                pair = RING + 2 * (use % 2)
                nc.vector.tensor_tensor(q_full[:, unit % 2, :], ps[:, pair, :], q_slot[:, unit % UNITS, :],
                                        ALU.add).then_inc(s_read, 1)

            def join_halves(index, read):
                dve.wait_ge(s_read, read)
                if not (isinstance(index, int) and index == 0):
                    dve.wait_ge(s_mcols, index)
                nc.vector.tensor_tensor(flat(neg_max[:]), half_max[:, 0, :], half_max[:, 1, :], ALU.min)\
                    .then_inc(s_neg, 1)

            def first_items():
                for n in range(SLOTS + LEAD):
                    dve.wait_ge(s_fill, n + 1)
                    if n == SLOTS:
                        dve.wait_ge(s_neg, 1)
                    reduce_item(n, n // SLOTS, n % SLOTS)
                    if n == SLOTS - 1:
                        join_halves(0, SLOTS)
                dve.wait_ge(s_fill, RING_BEFORE)
                place_max(SLOTS + LEAD, 0, None, 0)

            first_items()

            def body(i, first, last):
                base = ring_base(i)
                par0 = RING_BEFORE if first else RING_BEFORE - 1
                for r, kind, unit, item, n in ring_events(first, last):
                    dve.wait_ge(s_fill, base + n + 1)
                    use = par0 + n
                    if kind == "max":
                        if item == 0:
                            dve.wait_ge(s_neg, i * UNITS + unit)
                        reduce_item(use, unit, item)
                        if item == SLOTS - 1:
                            join_halves(i * UNITS + unit, base + n + 1)
                    elif kind == "turn_m":
                        if not (first and unit < 2):
                            dve.wait_ge(s_exp, i * (UNITS * 2 * SLOTS) + (unit - 1) * 2 * SLOTS)
                        place_max(use, unit, None, None)
                    else:
                        pair = RING + 2 * (use % 2)
                        ot = ps[:, pair, :].rearrange("p (q j r) -> p q j r", q=QT, r=STRIP)
                        step_no = i * UNITS + unit + 1
                        dve.wait_ge(s_read, base + n)
                        nc.vector.reciprocal(recip[:], ot[:, :, :, D]).then_inc(s_rec, 1)
                        dve.wait_ge(s_rec, step_no)
                        if unit < 0:
                            dst = attn[:, bass.ds(i - 1, 1), QT * (UNITS - 1):QT * UNITS, :]
                        else:
                            dst = attn[:, bass.ds(i, 1), QT * unit:QT * unit + QT, :]
                        dst = dst.rearrange("p a q (j d) -> p (a q) j d", d=D)
                        nc.vector.tensor_tensor(dst, ot[:, :, :, 0:D],
                                                recip[:].unsqueeze(3).to_broadcast([P, QT, HG, D]),
                                                ALU.mult).then_inc(s_read, 1)
            bodies(dve, body)

            PER = LN_STEPS + TOP_STEPS
            def experts(b):
                step, n_ = link(dve, s_moe, b * PER)
                hb = hid[:, bass.ds(b * TILES, TILES), :]
                for q in range(QUARTERS):
                    wait(dve, s_proj, b * QUARTERS + q + 1)
                    hq = hid[:, bass.ds(b * TILES + QT * q, QT), :]
                    nc.vector.tensor_tensor(hq, ps[:, 2 + q % 2, 0:QT * C].rearrange("p (t c) -> p t c", c=C),
                                            hq, ALU.add).then_inc(s_h1, 1)
                wait(dve, s_h1, b * QUARTERS + QUARTERS)
                layer_norm(dve, hb, xn[:], TILES, step, s_var, s_std, B + b + 1, s_xn)
                wait(dve, s_log, b * QUARTERS + QUARTERS)
                lg = ps[:, 4, 0:TILES * E].rearrange("p (t e) -> p t e", e=E)
                step(nc.vector.tensor_copy(logits[:], lg))

                def wide(a):
                    return a.unsqueeze(2).to_broadcast([P, TILES, E])
                ord_w = order[:].unsqueeze(1).to_broadcast([P, TILES, E])
                step(nc.vector.tensor_reduce(top[:], logits[:], AX.X, ALU.max))
                nc.vector.tensor_tensor(logits[:], logits[:], wide(top[:]), ALU.subtract).then_inc(s_shift, 1)
                wait(dve, s_pex, b + 1)
                step(nc.vector.reduce_sum(top[:], pr[:], AX.X))
                step(nc.vector.reciprocal(top[:], top[:]))
                step(nc.vector.tensor_tensor(pr[:], pr[:], wide(top[:]), ALU.mult))
                step(nc.vector.scalar_tensor_tensor(hot[:], logits[:], 0.0, ord_w, ALU.is_equal, ALU.mult))
                step(nc.vector.tensor_reduce(top[:], hot[:], AX.X, ALU.max))
                step(nc.vector.tensor_tensor(gate[:], ord_w, wide(top[:]), ALU.is_equal))
                step(nc.vector.scalar_tensor_tensor(logits[:], gate[:], -3.0e38, logits[:], ALU.mult, ALU.add))
                step(nc.vector.tensor_reduce(top[:], logits[:], AX.X, ALU.max))
                step(nc.vector.tensor_tensor(eq[:], logits[:], wide(top[:]), ALU.is_equal))
                step(nc.vector.tensor_tensor(hot[:], eq[:], ord_w, ALU.mult))
                step(nc.vector.tensor_reduce(top[:], hot[:], AX.X, ALU.max))
                step(nc.vector.tensor_tensor(eq[:], ord_w, wide(top[:]), ALU.is_equal))
                step(nc.vector.tensor_tensor(gate[:], gate[:], eq[:], ALU.add))
                step(nc.vector.tensor_tensor(gate[:], gate[:], pr[:], ALU.mult))
                step(nc.vector.reduce_sum(top[:], gate[:], AX.X))
                step(nc.vector.tensor_scalar(top[:], top[:], 1e-12, None, ALU.max))
                step(nc.vector.reciprocal(top[:], top[:]))
                nc.vector.tensor_tensor(gate[:], gate[:], wide(top[:]), ALU.mult).then_inc(s_gate, 1)
                assert n_[0] == PER, n_[0]
                for q in range(QUARTERS):
                    for pp in range(E // 2):
                        k = b * (QUARTERS * E // 2) + q * (E // 2) + pp
                        wait(dve, s_gelu, k + 1)
                        wait(dve, s_gb, k + 1)
                        if pp == 0:
                            wait(dve, s_down, b * QUARTERS + q)
                        nc.vector.tensor_tensor(gated[:, pp, :], ps[:, 2 + pp % 2, :], act_h[:, pp % 2, :],
                                                ALU.mult).then_inc(s_gated, 1)
                    wait(dve, s_down, b * QUARTERS + q + 1)
                    if q == 0:
                        wait(dve, s_out, b * 16)
                    rq = res[:, QT * q:QT * q + QT, :]
                    hq = hid[:, bass.ds(b * TILES + QT * q, QT), :]
                    nc.vector.tensor_tensor(rq, ps[:, 6, 0:QT * C].rearrange("p (t c) -> p t c", c=C), hq,
                                            ALU.add).then_inc(s_part, 1)
                    wait(dve, s_part, b * QUARTERS + q + 1)
                    ins = nc.vector.tensor_tensor(rq, rq, xn[:, QT * q:QT * q + QT, :], ALU.add)
                    if q == QUARTERS - 1:
                        ins.then_inc(s_res, 1)
            batches(dve, experts)

        @block.scalar
        def _(act):
            act.wait_ge(s_vones, 1)
            act.wait_ge(s_ones, 1)
            def project(b):
                wait(act, s_var, b + 1)
                nc.scalar.activation(lstd[:], lvar[:], ACT.Sqrt).then_inc(s_std, 1)
                for q in range(QUARTERS):
                    wait(act, s_xt, b * QUARTERS + q + 1)
                    nc.scalar.activation(xnT[0:C, q, :], ps[0:C, q, :], ACT.Copy).then_inc(s_xnT, 1)
                for q in range(QUARTERS):
                    n = q % 2
                    wait(act, s_qk, b * QUARTERS + q + 1)
                    wait(act, s_store[n], 16 * 2 * len(TERMS) * (b * 2 + q // 2))
                    nc.scalar.activation(part[:, n, 0, :], ps[:, 4 + n, :], ACT.Copy).then_inc(s_hi, 1)
                    wait(act, s_v, b * QUARTERS + q + 1)
                    for g in range(GROUPS):
                        src = ps[:, 6 + n, 0:QT * C].rearrange("p (t g j d) -> p g t j d", t=QT, g=GROUPS, j=HG)
                        dst = v_all[:, bass.ds(b * GROUPS + g, 1), QT * q:QT * q + QT, :]
                        dst = dst.rearrange("p a t (j w) -> p (a t) j w", w=VW)[:, :, :, 0:D]
                        ins = nc.scalar.activation(dst, src[:, g], ACT.Copy)
                    ins.then_inc(s_vfree, 1)
            batches(act, project)

            def body(i, first, last):
                total = UNITS * SLOTS
                turn = {u: n for _, kind, u, _, n in ring_events(first, last) if kind == "turn_o"}
                mid_turn = {u: n for _, kind, u, _, n in ring_events(False, False) if kind == "turn_o"}
                for r in range(total + (SLOTS if last else 0)):
                    if r < total:
                        for blk in (2 * r, 2 * r + 1):
                            kc, j = blk // HG, blk % HG
                            act.wait_ge(s_score, i * (2 * total) + blk + 1)
                            if j == 0 and not (first and kc < PBUF):
                                act.wait_ge(s_pv, i * (total // 2) + kc - PBUF + 1)
                            nc.scalar.activation(prob[:, kc % PBUF, j, :], ps[:, SCORE + blk % 3, :],
                                                 ACT.Exp).then_inc(s_exp, 1)
                    if r % SLOTS == O_EVAC and not (first and r < SLOTS) and r <= total + O_EVAC:
                        u = r // SLOTS - 1
                        act.wait_ge(s_pv, i * (total // 2) + TILES * (u + 1))
                        if u >= 1 or (u == 0 and not first):
                            prev = turn[u - 1]
                            act.wait_ge(s_fill, ring_base(i) + prev + 1)
                        elif u == -1 and not first:
                            if isinstance(i, int) or True:
                                act.wait_ge(s_fill, ring_base_prev(i, mid_turn[UNITS - 2]))
                        nc.scalar.activation(o_rows[:], ps[:, OBANK, :], ACT.Copy).then_inc(s_orow, 1)

            def ring_base_prev(i, n):
                return i * RING_PER_BODY - RING_PER_BODY + (RING_BEFORE - 1) + n + 1

            bodies(act, body)

            def experts(b):
                for q in range(QUARTERS):
                    wait(act, s_atT, b * QUARTERS + q + 1)
                    nc.scalar.activation(xnT[0:C, q, :], ps[0:C, q % 2, :], ACT.Copy).then_inc(s_atTr, 1)
                wait(act, s_var, B + b + 1)
                nc.scalar.activation(lstd[:], lvar[:], ACT.Sqrt).then_inc(s_std, 1)
                for q in range(QUARTERS):
                    wait(act, s_x2T, b * QUARTERS + q + 1)
                    nc.scalar.activation(xnT[0:C, q, :], ps[0:C, q % 2, :], ACT.Copy).then_inc(s_x2Tr, 1)
                wait(act, s_shift, b + 1)
                nc.scalar.activation(pr[:], logits[:], ACT.Exp).then_inc(s_pex, 1)
                for q in range(QUARTERS):
                    wait(act, s_gT, b * QUARTERS + q + 1)
                    nc.scalar.activation(gateT[:, q, :], ps[0:E, 5, :], ACT.Copy).then_inc(s_logr, 1)
                for q in range(QUARTERS):
                    for pp in range(E // 2):
                        k = b * (QUARTERS * E // 2) + q * (E // 2) + pp
                        wait(act, s_up, k + 1)
                        wait(act, s_gated, k - 1)
                        nc.scalar.activation(act_h[:, pp % 2, :], ps[:, pp % 2, :], ACT.Gelu).then_inc(s_gelu, 1)
            batches(act, experts)

        @block.tensor
        def _(pe):
            pe.wait_ge(s_w, 16 * 9)
            pe.wait_ge(s_const, 4)
            pe.wait_ge(s_zero, 2)
            pe.wait_ge(s_ones, 1)
            def project(b):
                wait(pe, s_xn, b + 1)
                wait(pe, s_xnT, b * QUARTERS)
                for q in range(QUARTERS):
                    stand_alone(pe)
                    for t in range(QT):
                        ins = nc.tensor.transpose(ps[0:C, q, P * t:P * t + P], xn[:, QT * q + t, :], ident[:])
                    ins.then_inc(s_xt, 1)
                for q in range(QUARTERS):
                    n = q % 2
                    wait(pe, s_xnT, b * QUARTERS + q + 1)
                    wait(pe, s_rest, b * QUARTERS + q - 1)
                    nc.tensor.matmul(ps[:, 4 + n, :], wqkv[:, 0:2 * C], xnT[:, q, :],
                                     start=True, stop=True).then_inc(s_qk, 1)
                    wait(pe, s_vfree, b * QUARTERS + q - 1)
                    for t in range(QT):
                        ins = nc.tensor.matmul(ps[:, 6 + n, C * t:C * t + C], xnT[:, q, P * t:P * t + P],
                                               wqkv[:, 2 * C:3 * C], start=True, stop=True)
                    ins.then_inc(s_v, 1)
            batches(pe, project)

            def max_item(use, unit, item):
                q, j, h = item // 8, (item // 2) % HG, item % 2
                key = (unit % UNITS) // 2
                for c in range(2):
                    ins = nc.tensor.matmul(ps[:, RING + 2 * (use % 2) + c, :],
                                           q_slot[:, unit % UNITS, P * q:P * q + P],
                                           k_slot[:, key, j, 1024 * h + 512 * c:1024 * h + 512 * c + 512],
                                           start=True, stop=True)
                ins.then_inc(s_fill, 1)

            def turn_max(use):
                for q in range(QT):
                    ins = nc.tensor.matmul(ps[:, RING + 2 * (use % 2), P * q:P * q + P], m_cols[:, q, :],
                                           ident16[:], start=True, stop=True)
                ins.then_inc(s_fill, 1)

            def turn_out(use):
                for q in range(QT):
                    ins = nc.tensor.transpose(ps[:, RING + 2 * (use % 2), P * q:P * q + P],
                                              o_rows[:, P * q:P * q + P], ident[:])
                ins.then_inc(s_fill, 1)

            pe.wait_ge(s_rest, B * QUARTERS)
            pe.wait_ge(s_vfree, B * QUARTERS)
            pe.wait_ge(s_kload[0], 16 * HG)
            pe.wait_ge(s_qload[0], 16 * HG)
            pe.wait_ge(s_qload[1], 16 * HG)
            for n in range(SLOTS + LEAD):
                if n >= 2:
                    pe.wait_ge(s_read, n - 1)
                max_item(n, n // SLOTS, n % SLOTS)
            pe.wait_ge(s_mcols, 1)
            pe.wait_ge(s_read, SLOTS + LEAD - 1)
            turn_max(SLOTS + LEAD)

            def body(i, first, last):
                base = ring_base(i)
                par0 = RING_BEFORE if first else RING_BEFORE - 1
                total = UNITS * SLOTS
                events = ring_events(first, last)
                loads = i * (16 * HG)
                for r in range(total + (SLOTS if last else 0)):
                    for _, kind, unit, item, n in [e for e in events if e[0] == r]:
                        use = par0 + n
                        pe.wait_ge(s_read, base + n - 1)
                        if kind == "max":
                            if item == 0:
                                pe.wait_ge(s_qload[unit % UNITS], loads + 16 * HG * (unit // UNITS + 1))
                                if unit % 2 == 0:
                                    pe.wait_ge(s_kload[(unit % UNITS) // 2], loads + 16 * HG * (unit // UNITS + 1))
                            max_item(use, unit, item)
                        elif kind == "turn_m":
                            pe.wait_ge(s_mcols, i * UNITS + unit + 1)
                            turn_max(use)
                        else:
                            pe.wait_ge(s_orow, i * UNITS + unit + 1)
                            turn_out(use)
                    if r < total:
                        unit = r // SLOTS
                        if r % SLOTS == 0:
                            if unit >= 1:
                                at = base + {v: n for _, k, v, _, n in events if k == "turn_m"}[unit] + 1
                            elif first:
                                at = RING_BEFORE
                            else:
                                at = base + {v: n for _, k, v, _, n in ring_events(False, False)
                                             if k == "turn_m"}[UNITS] + 1 - RING_PER_BODY
                            pe.wait_ge(s_read, at)
                        for blk in (2 * r, 2 * r + 1):
                            kc, j = blk // HG, blk % HG
                            if blk >= 3:
                                pe.wait_ge(s_exp, i * (2 * total) + blk - 2)
                            elif not first:
                                last_use = max(m for m in range(2 * total) if m % 3 == blk)
                                pe.wait_ge(s_exp, i * (2 * total) + last_use + 1 - 2 * total)
                            key = P * (kc % TILES)
                            nc.tensor.matmul(ps[:, SCORE + blk % 3, :],
                                             k_slot[:, (unit % UNITS) // 2, j, key:key + P],
                                             q_full[:, unit % 2, :], start=True, stop=True).then_inc(s_score, 1)
                    k = (r - PV_LAG) // 2
                    if (r - PV_LAG) % 2 == 0 and not (first and k < 0) and k < total // 2:
                        pe.wait_ge(s_exp, i * (2 * total) + HG * (k + 1))
                        kc = k % TILES
                        vs = ((k // TILES) % UNITS) // 2
                        if kc == 0:
                            if not (first and k == 0):
                                pe.wait_ge(s_orow, i * UNITS + k // TILES)
                            if (k // TILES) % 2 == 0:
                                pe.wait_ge(s_vload[vs], i + 1)
                        for j in range(HG):
                            lo = STRIP * j
                            ins = nc.tensor.matmul(ps[lo:lo + VW, OBANK, :],
                                                   v_slot[:, vs, kc, VW * j:VW * j + VW],
                                                   prob[:, k % PBUF, j, :],
                                                   start=(kc == 0), stop=(kc == TILES - 1),
                                                   tile_position=(0, lo))
                        ins.then_inc(s_pv, 1)
            bodies(pe, body)

            pe.wait_ge(s_read, ring_base(BG - 1) + len(ring_events(False, True)))
            def experts(b):
                for q in range(QUARTERS):
                    wait(pe, s_tok, b * QUARTERS + q + 1)
                    wait(pe, s_atTr, b * QUARTERS + q - 1)
                    if q == 0:
                        wait(pe, s_gelu, b * (QUARTERS * E // 2))
                        wait(pe, s_gated, b * (QUARTERS * E // 2))
                    stand_alone(pe)
                    for t in range(QT):
                        ins = nc.tensor.transpose(ps[0:C, q % 2, P * t:P * t + P], at_tok[:, q % 2, t, :], ident[:])
                    ins.then_inc(s_atT, 1)
                    wait(pe, s_atTr, b * QUARTERS + q + 1)
                    wait(pe, s_h1, b * QUARTERS + q - 1)
                    for t in range(QT):
                        ins = nc.tensor.matmul(ps[:, 2 + q % 2, C * t:C * t + C], xnT[:, q, P * t:P * t + P],
                                               wproj[:], start=True, stop=True)
                    ins.then_inc(s_proj, 1)
                wait(pe, s_xn, B + b + 1)
                for q in range(QUARTERS):
                    wait(pe, s_x2Tr, b * QUARTERS + q - 1)
                    stand_alone(pe)
                    for t in range(QT):
                        ins = nc.tensor.transpose(ps[0:C, q % 2, P * t:P * t + P], xn[:, QT * q + t, :], ident[:])
                    ins.then_inc(s_x2T, 1)
                for q in range(QUARTERS):
                    wait(pe, s_x2Tr, b * QUARTERS + q + 1)
                    for t in range(QT):
                        c = E * (QT * q + t)
                        ins = nc.tensor.matmul(ps[:, 4, c:c + E], xnT[0:C, q, P * t:P * t + P], wroute[:],
                                               start=True, stop=True)
                    ins.then_inc(s_log, 1)
                wait(pe, s_gate, b + 1)
                for q in range(QUARTERS):
                    wait(pe, s_logr, b * QUARTERS + q)
                    stand_alone(pe)
                    for t in range(QT):
                        ins = nc.tensor.transpose(ps[0:E, 5, P * t:P * t + P], gate[:, QT * q + t, :], ident[:])
                    ins.then_inc(s_gT, 1)
                wait(pe, s_logr, b * QUARTERS + QUARTERS)
                for q in range(QUARTERS):
                    for pp in range(E // 2):
                        k = b * (QUARTERS * E // 2) + q * (E // 2) + pp
                        wait(pe, s_gelu, k - 1)
                        nc.tensor.matmul(ps[:, pp % 2, :], w1s[:, P * pp:P * pp + P], xnT[:, q, :],
                                         start=True, stop=True).then_inc(s_up, 1)
                        wait(pe, s_gated, k - 1)
                        nc.tensor.matmul(ps[:, 2 + pp % 2, :], pick[:, pp, :], gateT[:, q, :],
                                         start=True, stop=True).then_inc(s_gb, 1)
                    k = b * (QUARTERS * E // 2) + q * (E // 2)
                    wait(pe, s_gated, k + E // 2)
                    wait(pe, s_part, b * QUARTERS + q)
                    for t in range(QT):
                        o = ps[:, 6, C * t:C * t + C]
                        for pp in range(E // 2):
                            nc.tensor.matmul(o, gated[:, pp, P * t:P * t + P], w2s[:, pp, :],
                                             start=(pp == 0), stop=False)
                        ins = nc.tensor.matmul(o, gateT[:, q, P * t:P * t + P], b2s[:], start=False, stop=True)
                    ins.then_inc(s_down, 1)
            batches(pe, experts)

_INS = ["x", "itok_BS_0_99998", "L0_tok_weight", "L0_attn_w_qkv", "L0_attn_b_qkv", "L0_attn_w_proj",
        "L0_attn_b_proj", "L0_ffn_router_w", "L0_ffn_w1", "L0_ffn_b1", "L0_ffn_w2", "L0_ffn_b2"]


def kernel(**inputs):
    import numpy as np
    import concourse.bacc as bacc
    from concourse.bass_utils import run_bass_kernel_spmd

    nc = bacc.Bacc("TRN2", target_bir_lowering=False, num_devices=1)
    arrays, args = {}, []
    for name in _INS:
        a = np.ascontiguousarray(inputs[name])
        arrays[f"in_{name}"] = a
        args.append(nc.dram_tensor(f"in_{name}", a.shape, mybir.dt.from_np(a.dtype), kind="ExternalInput").ap())
    out = nc.dram_tensor("out", (B, N, C), F32, kind="ExternalOutput").ap()
    build(nc, *args, out)
    r = run_bass_kernel_spmd(nc, [arrays], core_ids=[0])
    return r.results[0]["out"]
```

```python
from contextlib import ExitStack

import concourse.bass as bass
from concourse import mybir
from concourse.alu_op_type import AluOpType as ALU

ACT = mybir.ActivationFunctionType
AX = mybir.AxisListType
F32 = mybir.dt.float32
BF16 = mybir.dt.bfloat16
I32 = mybir.dt.int32

P = 128
VOCAB, C = 25000, 64
B, N = 4, 2048
H, D = 16, 4
E = 8
EPS = 1e-5

TILES = N // P
QUARTERS = 4
QT = TILES // QUARTERS
BLK = QT * P
BLOCKS = B * QUARTERS

GROUPS, HG = 4, 4
STRIP = 32
TERMS = [(0, 0), (0, 1), (0, 2), (1, 0), (1, 1), (2, 0)]
KROWS = D * len(TERMS)
PARTS = 3
STORES = 2 * len(TERMS)

UNITS = GROUPS
SLOTS = 32
BODY = UNITS * SLOTS
SCORES = 2 * BODY
CHUNKS = UNITS * TILES
LEAD = 10
PV_LAG = 5
PBUF = 4
VW = D + 1
SCORE_BANKS = 3

O_EVAC = 3
O_TURN = 9
M_TURN = 27
EMBED, LN1_SUM, LN1_VAR, TURN_X, QKV, STORE, GATHER = 0, 3, 7, 13, 17, 18, 90
TURN_A, PROJ, LN2_SUM, LN2_VAR, TURN_X2, ROUTER, SHIFT, NUMER, ROUTE, SPLIT_G = 11, 15, 19, 23, 29, 33, 35, 38, 43, 62
UP, TURN_G, PICK0, PICK1, DOWN = 49, 67, 71, 77, 85
ROUTES = 18

RING_KINDS = ("max", "turn_o", "turn_m", "turn_x", "qkv", "turn_a", "proj", "turn_x2", "router",
              "turn_g", "up0", "up1", "pick0", "pick1", "down")
PRO = [(EMBED, "embed"), (LN1_SUM, "ln1_sum"), (LN1_VAR, "ln1_var"), (TURN_X, "turn_x"), (QKV, "qkv"),
       (STORE, "store"), (GATHER, "gather")]
SOURCE = {"qkv": ("turn_x", 0), "turn_a": ("turn_o", -1), "proj": ("turn_a", 0), "router": ("turn_x2", 0),
          "pick0": ("turn_g", 0), "pick1": ("turn_g", 0), "down": ("pick1", 0)}
MOE = [(TURN_A, "turn_a"), (PROJ, "proj"), (LN2_SUM, "ln2_sum"), (LN2_VAR, "ln2_var"),
       (TURN_X2, "turn_x2"), (ROUTER, "router"), (SHIFT, "shift"), (NUMER, "numer"),
       *((ROUTE + n, "route", n) for n in range(UP - ROUTE)), (UP, "up0"), (UP, "up1"),
       *((ROUTE + n, "route", n) for n in range(UP - ROUTE, ROUTES)), (SPLIT_G, "split_g"),
       (TURN_G, "turn_g"), (PICK0, "pick0"), (PICK1, "pick1"), (DOWN, "down")]


def events_of(first, last, pro, moe):
    out = []
    for r in range(BODY + (SLOTS if last else 0)):
        ahead = r + SLOTS + LEAD
        if not (last and ahead >= BODY):
            out.append((r, "max", ahead // SLOTS, ahead % SLOTS))
        u = r // SLOTS
        if r % SLOTS == O_TURN and not (first and u == 0) and u <= UNITS:
            out.append((r, "turn_o", u - 1, 0))
        if r % SLOTS == M_TURN and not (last and u + 1 >= UNITS):
            out.append((r, "turn_m", u + 1, 0))
        out += [(r, kind, 0, *(step or [0])) for at, kind, *step in PRO if pro and at == r]
        out += [(r, kind, 0, *(step or [0])) for at, kind, *step in MOE if moe and at == r]
    return out


class Part:

    def __init__(self, start, stop, events, at_ring, at_read, first=False, last=False):
        self.start, self.stop, self.events, self.first, self.last = start, stop, events, first, last
        self.at_ring, self.at_read = at_ring, at_read
        self.ring, self.read = [], []
        ring = read = 0
        for e in events:
            self.ring.append(ring)
            self.read.append(read)
            if e[1] in RING_KINDS:
                ring += 1
                read += e[1] not in ("up0", "up1")
        self.rings, self.reads = ring, read

    def ring_at(self, i, n):
        return self.counted(i, self.rings, self.at_ring + self.ring[n])

    def read_at(self, i, n):
        return self.counted(i, self.reads, self.at_read + self.read[n])

    def counted(self, i, each, at):
        return i * each + (at - self.start * each) if self.start != self.stop else at

    def find(self, kind, unit=0, item=0):
        for n, e in enumerate(self.events):
            if e[1:] == (kind, unit, item):
                return n
        raise KeyError((kind, unit, item))

    def after(self):
        turns = max(self.stop - self.start, 1)
        return self.at_ring + turns * self.rings, self.at_read + turns * self.reads


def plan():
    parts, at = [], (0, 0)

    def add(start, stop, events, **kw):
        nonlocal at
        parts.append(Part(start, stop, events, *at, **kw))
        at = parts[-1].after()

    add(0, QUARTERS, [(0, kind, 0, *(step or [0])) for _, kind, *step in PRO])
    head = [(n, "max", n // SLOTS, n % SLOTS) for n in range(SLOTS + LEAD)] + [(SLOTS + LEAD, "turn_m", 0, 0)]
    add(0, 0, head)
    add(0, 0, events_of(True, False, True, False), first=True)
    with_pro = BLOCKS - QUARTERS
    add(1, with_pro, events_of(False, False, True, True))
    add(with_pro, BLOCKS - 1, events_of(False, False, False, True))
    add(BLOCKS - 1, BLOCKS - 1, events_of(False, True, False, True), last=True)
    add(BLOCKS, BLOCKS, [(0, kind, 0, *(step or [0])) for _, kind, *step in MOE])
    for p in parts:
        assert p.stop - p.start <= 1 or p.rings % 2 == 0
    return parts


PROLOGUE, HEAD, *BODIES, TAIL = plan()


def run_bodies(eng, emit):
    for part in BODIES:
        if part.stop == part.start:
            emit(part, part.start)
        else:
            with eng.Fori(part.start, part.stop) as i:
                emit(part, i)


def run_prologue(eng, emit):
    emit(PROLOGUE, 0)
    with eng.Fori(1, QUARTERS) as x:
        emit(PROLOGUE, x)


def above_zero(value):
    return not isinstance(value, int) or value > 0


def build(nc, x, itok, table, w_qkv, b_qkv, w_proj, b_proj, router_w, w1, b1, w2, b2, out):
    with ExitStack() as ctx:
        def sb(name, shape, dt=F32):
            return ctx.enter_context(nc.sbuf_tensor(name, shape, dt))

        def sem(name):
            return ctx.enter_context(nc.semaphore(name))

        q_rows = nc.dram_tensor("q_rows", (BLOCKS, GROUPS, P, BLK), BF16, kind="Internal").ap()
        k_rows = nc.dram_tensor("k_rows", (B, GROUPS, P, N), BF16, kind="Internal").ap()

        ps = ctx.enter_context(nc.psum_tensor("ps", [P, 8, 512], F32))
        SCORE, OBANK = 4, 7

        ident = sb("ident", [P, P])
        ident16 = sb("ident16", [P, P], BF16)
        wqkv = sb("wqkv", [C + 1, 3 * C])
        wproj = sb("wproj", [C + 1, C])
        wroute = sb("wroute", [C, E])
        w1s = sb("w1s", [C + 1, E * C])
        w2s = sb("w2s", [P, E // 2, C])
        b2s = sb("b2s", [PARTS * E, C])
        b2r = sb("b2r", [PARTS * E, C])
        b2p = sb("b2p", [PARTS * E, PARTS, C], BF16)
        pick = sb("pick", [PARTS * E, E // 2, P], BF16)
        minus_half = sb("minus_half", [P, QT])
        order = sb("order", [P, E])

        ids = sb("ids", [P, 2, B * TILES], I32)
        idsf = sb("idsf", [P, 2, B * TILES])
        negf = sb("negf", [P, 2, B * TILES])
        rows = sb("rows", [P, 2, B * TILES + QT], I32)
        differ_i = sb("differ_i", [P, B * TILES], I32)
        differ = sb("differ", [P, B * TILES])
        hid = sb("hid", [P, B * TILES, C])
        v_all = sb("v_all", [P, BLOCKS, QT, H * VW])

        row_now = sb("row_now", [P, 2, QT], I32)
        emb = sb("emb", [P, 2, QT, C])
        h0 = sb("h0", [P, QT, C])
        ln = [{k: sb(f"ln{n}_{k}", [P, QT] if k in ("sum", "var", "y", "t") else [P, QT, C])
               for k in ("sum", "var", "y", "t", "xc", "sq", "xn")} for n in (1, 2)]
        xT = sb("xT", [C + 1, BLK])
        part = sb("part", [P, PARTS, BLK], BF16)
        rest = sb("rest", [P, BLK])

        k_slot = sb("k_slot", [P, GROUPS, HG, N], BF16)
        q_slot = sb("q_slot", [P, UNITS, BLK], BF16)
        v_slot = sb("v_slot", [P, GROUPS, TILES, HG * VW])
        q_full = sb("q_full", [P, 2, BLK], BF16)
        prob = sb("prob", [P, PBUF, HG, BLK])
        half_max = sb("half_max", [P, 2, 2, QT * HG])
        neg_max = sb("neg_max", [P, QT, HG])
        rest_max = sb("rest_max", [P, QT, HG])
        m_cols = sb("m_cols", [P, QT, P], BF16)
        o_rows = sb("o_rows", [P, BLK])
        recip = sb("recip", [P, QT, HG])
        attn = sb("attn", [P, QT, C])

        aT = sb("aT", [C + 1, BLK])
        h1 = sb("h1", [P, QT, C])
        x2T = sb("x2T", [C + 1, BLK])
        logits = sb("logits", [P, QT, E])
        top = sb("top", [P, QT])
        pr = sb("pr", [P, QT, E])
        gate = sb("gate", [P, QT, E])
        hot = sb("hot", [P, QT, E])
        g_rest = sb("g_rest", [P, QT, E])
        g_cols = sb("g_cols", [P, QT, PARTS * E], BF16)
        gT = sb("gT", [PARTS * E, BLK], BF16)
        act_h = sb("act_h", [P, 2, 2, BLK])
        gated = sb("gated", [P, E // 2, BLK])
        res = sb("res", [P, QT, C])

        s_passed = sem("waits_passed")
        s_zeroed = sem("pool_zeroed")
        s_const = sem("constants_ready")
        s_w = sem("weights_loaded")
        s_b2 = sem("b2_steps")
        s_ones = sem("token_ones_ready")
        s_kzero = sem("key_slots_zero")
        s_kones = sem("key_strips_one")
        s_opsum = sem("output_bank_zeroed")
        s_ids = sem("ids_loaded")
        s_idstep = sem("id_steps")
        s_row = sem("rows_ready")
        s_rownow = sem("row_now_ready")
        s_gather = sem("gathered")
        s_mask = sem("second_masked")
        s_emb = sem("embedded")
        s_hid = sem("hidden_kept")
        s_sum = [sem(f"ln{n}_sum_ready") for n in (1, 2)]
        s_sq = [sem(f"ln{n}_squares_ready") for n in (1, 2)]
        s_var = [sem(f"ln{n}_var_steps") for n in (1, 2)]
        s_lnp = [sem(f"ln{n}_pool_steps") for n in (1, 2)]
        s_xn = [sem(f"ln{n}_ready") for n in (1, 2)]
        s_hi = sem("hi_ready")
        s_rest = sem("rest_ready")
        s_mid = sem("mid_ready")
        s_lo = sem("lo_ready")
        s_store = sem("rows_stored")
        s_kload = [sem(f"k_loaded_{n}") for n in range(GROUPS)]
        s_qload = [sem(f"q_loaded_{n}") for n in range(UNITS)]
        s_vload = [sem(f"v_copied_{n}") for n in range(GROUPS)]
        s_fill = sem("ring_filled")
        s_read = sem("ring_read")
        s_neg = sem("neg_max_ready")
        s_pmax = sem("max_steps")
        s_mcols = sem("m_cols_ready")
        s_score = sem("scores_filled")
        s_exp = sem("exps_done")
        s_pv = sem("pv_done")
        s_orow = sem("o_rows_ready")
        s_rec = sem("recip_ready")
        s_shift = sem("logits_shifted")
        s_route = sem("route_steps")
        s_pex = sem("numerators_ready")
        s_gstep = sem("gate_steps")
        s_gcols = sem("gate_cols_ready")
        s_gelu = sem("gelu_ready")
        s_res = sem("result_ready")
        s_free = sem("result_buffer_free")

        block = ctx.enter_context(nc.Block())

        def flat(ap):
            return ap.rearrange("p a b -> p (a b)")

        def stand_alone(eng):
            eng.sem_inc(s_passed, 1)

        def link(eng, s, base):
            n = [0]

            def step(ins):
                n[0] += 1
                ins.then_inc(s, 1)
                eng.wait_ge(s, base + n[0])
            return step, n

        def turn_of(p, i, kind):
            if kind in [e[1] for e in MOE]:
                return i - 1
            return i if p is PROLOGUE else i + QUARTERS

        LNP_STEPS, VAR_STEPS, ROUTE_STEPS, MAX_STEPS = 7, 1, 2 + ROUTES, 3

        @block.sync
        def _(sp):
            for n, src in enumerate((x, itok)):
                sp.dma_start(ids[:, n, :].rearrange("p (b t) -> p b t", b=B),
                             src.rearrange("b (p t) -> p b t", p=P)).then_inc(s_ids, 16)
            loads = [
                (wqkv[0:C, :], w_qkv),
                (wqkv[C:C + 1, :], b_qkv.rearrange("(a n) -> a n", a=1)),
                (wproj[0:C, :], w_proj),
                (wproj[C:C + 1, :], b_proj.rearrange("(a n) -> a n", a=1)),
                (w1s[0:C, :].rearrange("i (e o) -> i e o", e=E), w1.rearrange("e i o -> i e o")),
                (w1s[C:C + 1, :], b1.rearrange("(a e) o -> a (e o)", a=1)),
                (w2s[:], w2.rearrange("(r e) i o -> (e i) r o", e=2)),
            ] + [(b2s[E * n:E * n + E, :], b2) for n in range(PARTS)]
            for dst, src in loads:
                sp.dma_start(dst, src).then_inc(s_w, 16)
            sp.dma_start(wroute[:], router_w.rearrange("e c -> c e"),
                         allow_slow_non_contiguous=True).then_inc(s_w, 16)
            sp.sem_inc(s_free, 16)

            def store_rows(xb):
                sp.wait_ge(s_lo, xb + 1)
                for t, (pq, pk) in enumerate(TERMS):
                    qd = q_rows[bass.ds(xb, 1), :, :, :]
                    kd = k_rows[bass.ds(xb // QUARTERS, 1), :, :, bass.ds(xb % QUARTERS * BLK, BLK)]
                    for dst, side, p0 in ((qd, pq, 0), (kd, pk, C)):
                        d = dst.rearrange("a g (j r) n -> (a g) j r n", r=STRIP)[:, :, D * t:D * t + D, :]
                        sp.dma_start(d, part[p0:p0 + C, side, :]).then_inc(s_store, 16)

            def load_k(g, i):
                for j in range(HG):
                    lo = STRIP * j
                    sp.dma_start(k_slot[lo:lo + KROWS, g, j, :],
                                 k_rows[bass.ds(i // QUARTERS, 1), g, lo:lo + KROWS, :]
                                 .rearrange("a r n -> (a r) n")).then_inc(s_kload[g], 16)

            def load_q(u, i):
                for j in range(HG):
                    lo = STRIP * j
                    sp.dma_start(q_slot[lo:lo + KROWS, u, :],
                                 q_rows[bass.ds(i, 1), u, lo:lo + KROWS, :].rearrange("a r n -> (a r) n"))\
                        .then_inc(s_qload[u], 16)

            run_prologue(sp, lambda p, xb: store_rows(xb))
            sp.wait_ge(s_store, 16 * STORES * QUARTERS)
            sp.wait_ge(s_kones, HG)
            sp.wait_ge(s_const, 4)
            for u in range(UNITS):
                load_q(u, 0)
                load_k(u, 0)

            def body(p, i):
                if any(e[1] == "store" for e in p.events):
                    store_rows(i + QUARTERS)
                    sp.wait_ge(s_store, (i + QUARTERS + 1) * (16 * STORES))
                for u in range(UNITS if not p.last else 0):
                    sp.wait_ge(s_exp, i * SCORES + (u + 1) * 2 * SLOTS)
                    load_q(u, i + 1)
                    load_k(u, i + 1)
                    if u == 1 and not p.first:
                        store_out(i - 1)
                if p.last:
                    store_out(i - 1)

            def store_out(m):
                sp.wait_ge(s_res, m + 1)
                dst = out[bass.ds(m // QUARTERS, 1), :, :].rearrange("a (p q t) c -> (a p) q (t c)", p=P, q=QUARTERS)
                sp.dma_start(dst[:, bass.ds(m % QUARTERS, 1), :],
                             res[:].rearrange("p t c -> p (t c)").unsqueeze(1)).then_inc(s_free, 16)

            run_bodies(sp, body)
            store_out(BLOCKS - 1)
            sp.wait_ge(s_free, 16 * (BLOCKS + 1))

        @block.gpsimd
        def _(pool):
            nc.gpsimd.memset(ident[:], 0.0).then_inc(s_zeroed, 1)
            nc.gpsimd.memset(ident16[:], 0.0).then_inc(s_zeroed, 1)
            nc.gpsimd.memset(pick[:], 0.0).then_inc(s_zeroed, 1)
            nc.gpsimd.memset(q_slot[:], 0.0).then_inc(s_const, 1)
            nc.gpsimd.memset(m_cols[:], 0.0).then_inc(s_const, 1)
            nc.gpsimd.memset(minus_half[:], -0.5).then_inc(s_const, 1)
            nc.gpsimd.iota(order[:], [[-1, E]], base=E, channel_multiplier=0,
                           allow_small_or_imprecise_dtypes=True).then_inc(s_const, 1)

            def gather(xb):
                nc.gpsimd.tensor_copy(row_now[:], rows[:, :, bass.ds(xb * QT, QT)]).then_inc(s_rownow, 1)
                pool.wait_ge(s_rownow, xb + 1)
                stand_alone(pool)
                for t in range(QT):
                    for n in range(2):
                        nc.gpsimd.indirect_dma_start(
                            out=emb[:, n, t, :], out_offset=None, in_=table,
                            in_offset=bass.IndirectOffsetOnAxis(ap=row_now[:, n, t:t + 1], axis=0))\
                            .then_inc(s_gather, 16)

            def embed(xb):
                pool.wait_ge(s_gather, (xb + 1) * (2 * QT * 16))
                mask = differ[:, bass.ds(xb * QT, QT)].unsqueeze(2).to_broadcast([P, QT, C])
                nc.gpsimd.tensor_tensor(emb[:, 1, :, :], emb[:, 1, :, :], mask, ALU.mult).then_inc(s_mask, 1)
                pool.wait_ge(s_mask, xb + 1)
                nc.gpsimd.tensor_tensor(h0[:], emb[:, 0, :, :], emb[:, 1, :, :], ALU.add).then_inc(s_emb, 1)
                pool.wait_ge(s_emb, xb + 1)
                stand_alone(pool)
                nc.gpsimd.tensor_copy(hid[:, bass.ds(xb * QT, QT), :], h0[:]).then_inc(s_hid, 1)

            def wide(a):
                return a.unsqueeze(2).to_broadcast([P, QT, C])

            def ln_squares(w, src, k):
                step, _ = link(pool, s_lnp[w], k * LNP_STEPS)
                pool.wait_ge(s_sum[w], k + 1)
                stand_alone(pool)
                step(nc.gpsimd.tensor_scalar(ln[w]["t"][:], ln[w]["sum"][:], -1.0 / C, 0.0, ALU.mult, ALU.add))
                step(nc.gpsimd.tensor_tensor(ln[w]["xc"][:], src[:], wide(ln[w]["t"][:]), ALU.add))
                nc.gpsimd.tensor_tensor(ln[w]["sq"][:], ln[w]["xc"][:], ln[w]["xc"][:], ALU.mult)\
                    .then_inc(s_sq[w], 1)

            def ln_scale(w, k):
                step, n = link(pool, s_lnp[w], k * LNP_STEPS + 2)
                pool.wait_ge(s_var[w], (k + 1) * (VAR_STEPS + 1))
                t, y, v = (ln[w][a] for a in ("t", "y", "var"))
                step(nc.gpsimd.tensor_tensor(y[:], v[:], minus_half[:], ALU.pow))
                step(nc.gpsimd.tensor_tensor(t[:], y[:], y[:], ALU.mult))
                step(nc.gpsimd.tensor_tensor(t[:], t[:], v[:], ALU.mult))
                stand_alone(pool)
                step(nc.gpsimd.tensor_scalar(t[:], t[:], -0.5, 1.5, ALU.mult, ALU.add))
                step(nc.gpsimd.tensor_tensor(y[:], y[:], t[:], ALU.mult))
                nc.gpsimd.tensor_tensor(ln[w]["xn"][:], ln[w]["xc"][:], wide(y[:]), ALU.mult).then_inc(s_xn[w], 1)
                assert n[0] + 2 == LNP_STEPS

            def split_qk(xb):
                pool.wait_ge(s_rest, xb + 1)
                stand_alone(pool)
                nc.gpsimd.tensor_copy(part[:, 1, :], rest[:]).then_inc(s_mid, 1)
                pool.wait_ge(s_mid, xb + 1)
                nc.gpsimd.tensor_tensor(part[:, 2, :], rest[:], part[:, 1, :], ALU.subtract).then_inc(s_lo, 1)

            def copy_v(g, i):
                src = v_all[:, bass.ds(i // QUARTERS * QUARTERS, QUARTERS), :, g * HG * VW:(g + 1) * HG * VW]
                stand_alone(pool)
                nc.gpsimd.tensor_copy(v_slot[:, g, :, :].rearrange("p (q t) v -> p q t v", q=QUARTERS), src)\
                    .then_inc(s_vload[g], 1)

            def split_max(index, turned):
                step, _ = link(pool, s_pmax, index * MAX_STEPS)
                pool.wait_ge(s_neg, index + 1)
                if above_zero(turned):
                    pool.wait_ge(s_fill, turned)
                cols = m_cols[:].rearrange("p q (j r) -> p q j r", r=STRIP)
                stand_alone(pool)
                step(nc.gpsimd.tensor_copy(cols[:, :, :, KROWS], neg_max[:]))
                step(nc.gpsimd.tensor_tensor(rest_max[:], neg_max[:], cols[:, :, :, KROWS], ALU.subtract))
                stand_alone(pool)
                step(nc.gpsimd.tensor_copy(cols[:, :, :, KROWS + 1], rest_max[:]))
                nc.gpsimd.tensor_tensor(cols[:, :, :, KROWS + 2], rest_max[:], cols[:, :, :, KROWS + 1],
                                        ALU.subtract).then_inc(s_mcols, 1)

            def split_gates(m):
                step, _ = link(pool, s_gstep, m * MAX_STEPS)
                pool.wait_ge(s_route, (m + 1) * ROUTE_STEPS)
                stand_alone(pool)
                step(nc.gpsimd.tensor_copy(g_cols[:, :, 0:E], gate[:]))
                step(nc.gpsimd.tensor_tensor(g_rest[:], gate[:], g_cols[:, :, 0:E], ALU.subtract))
                stand_alone(pool)
                step(nc.gpsimd.tensor_copy(g_cols[:, :, E:2 * E], g_rest[:]))
                nc.gpsimd.tensor_tensor(g_cols[:, :, 2 * E:3 * E], g_rest[:], g_cols[:, :, E:2 * E],
                                        ALU.subtract).then_inc(s_gcols, 1)

            def side(p, i, kind):
                k = turn_of(p, i, kind)
                if kind == "embed":
                    embed(k)
                elif kind == "ln1_sum":
                    ln_squares(0, h0, k)
                elif kind == "ln1_var":
                    ln_scale(0, k)
                elif kind == "qkv":
                    split_qk(k)
                elif kind == "ln2_sum":
                    ln_squares(1, h1, k)
                elif kind == "ln2_var":
                    ln_scale(1, k)
                elif kind == "split_g":
                    split_gates(k)

            pool.wait_ge(s_row, 1)
            gather(0)
            pool.wait_ge(s_zeroed, 3)
            for m in (ident, ident16):
                nc.gpsimd.affine_select(out=m[:], in_=m[:], compare_op=ALU.not_equal, fill=1.0, base=0,
                                        pattern=[[-1, P]], channel_multiplier=1).then_inc(s_const, 1)
            for n in range(PARTS):
                for e in range(2):
                    half = pick[:, :, C * e:C * e + C]
                    nc.gpsimd.affine_select(out=half, in_=half, compare_op=ALU.not_equal, fill=1.0,
                                            base=-(E * n + e), pattern=[[-2, E // 2], [0, C]],
                                            channel_multiplier=1).then_inc(s_const, 1)
                    pool.wait_ge(s_const, 6 + 2 * n + e + 1)
            pool.wait_ge(s_w, 16 * 11)
            step, _ = link(pool, s_b2, 0)
            step(nc.gpsimd.memset(b2p[:], 0.0))
            step(nc.gpsimd.tensor_copy(b2p[:, 0, :], b2s[:]))
            step(nc.gpsimd.tensor_tensor(b2r[:], b2s[:], b2p[:, 0, :], ALU.subtract))
            step(nc.gpsimd.tensor_copy(b2p[:, 1, :], b2r[:]))
            step(nc.gpsimd.tensor_tensor(b2p[:, 2, :], b2r[:], b2p[:, 1, :], ALU.subtract))

            def prologue(p, xb):
                for _, kind, _, _ in p.events:
                    side(p, xb, kind)
                    if kind == "ln1_var":
                        gather(xb + 1)
            run_prologue(pool, prologue)

            pool.wait_ge(s_read, HEAD.at_read)
            for g in range(GROUPS):
                copy_v(g, 0)
            split_max(0, 0)

            def body(p, i):
                n_turn = {e[2]: n for n, e in enumerate(p.events) if e[1] == "turn_m"}
                for n, (r, kind, unit, item) in enumerate(p.events):
                    if kind == "max" and item == SLOTS - 1:
                        if unit - 1 in n_turn:
                            turned = p.ring_at(i, n_turn[unit - 1]) + 1
                        elif p.first:
                            turned = HEAD.at_ring + HEAD.rings
                        else:
                            left = BODY - (SLOTS * (UNITS - 1) + M_TURN) - 1
                            turned = p.ring_at(i, 0) - left
                        split_max(i * UNITS + unit, turned)
                    if kind == "gather":
                        gather(i + QUARTERS + 1)
                    side(p, i, kind)
                    if kind == "max" and r % SLOTS == 12 and item is not None:
                        g = r // SLOTS - 1
                        if g >= 0 and not p.last and g < UNITS - 1:
                            pool.wait_ge(s_pv, i * CHUNKS + (g + 1) * TILES)
                            copy_v(g, i + 1)
                        if g == -1 and not p.first:
                            pool.wait_ge(s_pv, i * CHUNKS)
                            copy_v(UNITS - 1, i)

            run_bodies(pool, body)
            for _, kind, _, _ in TAIL.events:
                side(TAIL, BLOCKS, kind)
            pool.wait_ge(s_gather, (BLOCKS + 1) * 2 * QT * 16)

        @block.vector
        def _(dve):
            dve.wait_ge(s_ids, 32)
            step, _ = link(dve, s_idstep, 0)
            step(nc.vector.tensor_copy(idsf[:], ids[:]))
            step(nc.vector.tensor_scalar(negf[:], idsf[:], 0.0, float(VOCAB), ALU.is_lt, ALU.mult))
            step(nc.vector.tensor_tensor(idsf[:], idsf[:], negf[:], ALU.add))
            step(nc.vector.tensor_scalar(idsf[:], idsf[:], 0.0, float(VOCAB - 1), ALU.max, ALU.min))
            step(nc.vector.memset(rows[:], 0))
            step(nc.vector.tensor_copy(rows[:, :, 0:B * TILES], idsf[:]))
            step(nc.vector.tensor_tensor(differ_i[:], ids[:, 0, :], ids[:, 1, :], ALU.bitwise_xor))
            nc.vector.tensor_scalar(differ[:], differ_i[:], 0.0, None, ALU.not_equal).then_inc(s_row, 1)
            for t in (xT, aT, x2T):
                nc.vector.memset(t[:], 1.0).then_inc(s_ones, 1)
            nc.vector.memset(v_all[:], 1.0).then_inc(s_ones, 1)
            nc.vector.memset(ps[:, OBANK, :], 0.0).then_inc(s_opsum, 1)
            nc.vector.memset(k_slot[:].rearrange("p g j n -> p (g j n)").bitcast(F32), 0.0).then_inc(s_kzero, 1)
            dve.wait_ge(s_ones, 4)

            def ln_sum(w, src, k):
                nc.vector.reduce_sum(ln[w]["sum"][:], src[:], AX.X).then_inc(s_sum[w], 1)

            def ln_var(w, k):
                step, _ = link(dve, s_var[w], k * (VAR_STEPS + 1))
                dve.wait_ge(s_sq[w], k + 1)
                step(nc.vector.reduce_sum(ln[w]["var"][:], ln[w]["sq"][:], AX.X))
                nc.vector.tensor_scalar(ln[w]["var"][:], ln[w]["var"][:], 1.0 / C, EPS, ALU.mult, ALU.add)\
                    .then_inc(s_var[w], 1)

            def wide(a):
                return a.unsqueeze(2).to_broadcast([P, QT, E])

            def route(m, n):
                lg, g = logits[:], gate[:]
                by_order = order[:].unsqueeze(1).to_broadcast([P, QT, E])
                if n == 0:
                    dve.wait_ge(s_pex, m + 1)
                else:
                    dve.wait_ge(s_route, m * ROUTE_STEPS + 2 + n)
                if n == 0:
                    ins = nc.vector.reduce_sum(top[:], pr[:], AX.X)
                elif n == 1:
                    ins = nc.vector.reciprocal(top[:], top[:])
                elif n == 2:
                    ins = nc.vector.tensor_tensor(pr[:], pr[:], wide(top[:]), ALU.mult)
                elif n == 3:
                    ins = nc.vector.scalar_tensor_tensor(hot[:], lg, 0.0, by_order, ALU.is_equal, ALU.mult)
                elif n == 4:
                    ins = nc.vector.tensor_reduce(top[:], hot[:], AX.X, ALU.max)
                elif n == 5:
                    ins = nc.vector.tensor_tensor(g, by_order, wide(top[:]), ALU.is_equal)
                elif n == 6:
                    ins = nc.vector.scalar_tensor_tensor(lg, g, -3.0e38, lg, ALU.mult, ALU.add)
                elif n == 7:
                    ins = nc.vector.tensor_reduce(top[:], lg, AX.X, ALU.max)
                elif n == 8:
                    ins = nc.vector.tensor_tensor(hot[:], lg, wide(top[:]), ALU.is_equal)
                elif n == 9:
                    ins = nc.vector.tensor_tensor(hot[:], hot[:], by_order, ALU.mult)
                elif n == 10:
                    ins = nc.vector.tensor_reduce(top[:], hot[:], AX.X, ALU.max)
                elif n == 11:
                    ins = nc.vector.tensor_tensor(hot[:], by_order, wide(top[:]), ALU.is_equal)
                elif n == 12:
                    ins = nc.vector.tensor_tensor(g, g, hot[:], ALU.add)
                elif n == 13:
                    ins = nc.vector.tensor_tensor(g, g, pr[:], ALU.mult)
                elif n == 14:
                    ins = nc.vector.reduce_sum(top[:], g, AX.X)
                elif n == 15:
                    ins = nc.vector.tensor_scalar(top[:], top[:], 1e-12, None, ALU.max)
                elif n == 16:
                    ins = nc.vector.reciprocal(top[:], top[:])
                else:
                    ins = nc.vector.tensor_tensor(g, g, wide(top[:]), ALU.mult)
                ins.then_inc(s_route, 1)

            def by_tile(bank, width):
                return ps[:, bank, 0:QT * width].rearrange("p (t c) -> p t c", c=width)

            def join(index, parity, done):
                dve.wait_ge(s_read, done)
                if above_zero(index):
                    dve.wait_ge(s_mcols, index)
                halves = half_max[:, parity, :, :]
                nc.vector.tensor_tensor(flat(neg_max[:]), halves[:, 0, :], halves[:, 1, :], ALU.min)\
                    .then_inc(s_neg, 1)

            def event(p, i, n):
                r, kind, unit, item = p.events[n]
                k = turn_of(p, i, kind)
                use = p.at_ring + p.ring[n]
                bank = 2 * (use % 2)
                done = p.read_at(i, n) + 1
                if kind in RING_KINDS and kind not in ("up0", "up1"):
                    dve.wait_ge(s_fill, p.ring_at(i, n) + 1)
                if kind == "max":
                    q, j, h = item // 8, (item // 2) % HG, item % 2
                    nc.vector.tensor_reduce(half_max[:, unit % 2, h, HG * q + j:HG * q + j + 1],
                                            ps[:, bank:bank + 2, :], AX.XY, ALU.max, negate=True).then_inc(s_read, 1)
                    if item == 0 and p is not HEAD:
                        join(i * UNITS + unit - 1, (unit - 1) % 2, done - 1)
                    elif item == 0 and unit == 1:
                        join(0, 0, done - 1)
                    elif item == SLOTS - 1 and p.last and unit == UNITS - 1:
                        join(i * UNITS + unit, unit % 2, done)
                elif kind == "turn_m":
                    if not (p is HEAD or p.first and unit < 2):
                        dve.wait_ge(s_exp, i * SCORES + (unit - 1) * 2 * SLOTS)
                    nc.vector.tensor_tensor(q_full[:, unit % 2, :], ps[:, bank, :], q_slot[:, unit % UNITS, :],
                                            ALU.add).then_inc(s_read, 1)
                elif kind == "turn_o":
                    ot = ps[:, bank, :].rearrange("p (q j r) -> p q j r", q=QT, r=STRIP)
                    dve.wait_ge(s_read, done - 1)
                    nc.vector.reciprocal(recip[:], ot[:, :, :, D]).then_inc(s_rec, 1)
                    dve.wait_ge(s_rec, i * UNITS + unit + 1)
                    g = unit % UNITS
                    dst = attn[:, :, g * HG * D:(g + 1) * HG * D].rearrange("p q (j d) -> p q j d", d=D)
                    nc.vector.tensor_tensor(dst, ot[:, :, :, 0:D],
                                            recip[:].unsqueeze(3).to_broadcast([P, QT, HG, D]),
                                            ALU.mult).then_inc(s_read, 1)
                elif kind == "ln1_sum":
                    dve.wait_ge(s_emb, k + 1)
                    stand_alone(dve)
                    ln_sum(0, h0, k)
                elif kind == "ln1_var":
                    ln_var(0, k)
                elif kind == "turn_x":
                    nc.vector.tensor_copy(xT[0:C, :], ps[0:C, bank, :]).then_inc(s_read, 1)
                elif kind == "qkv":
                    if above_zero(k):
                        dve.wait_ge(s_store, k * (16 * STORES))
                    nc.vector.tensor_copy(part[:, 0, :], ps[:, bank, :]).then_inc(s_hi, 1)
                    dve.wait_ge(s_hi, k + 1)
                    nc.vector.tensor_tensor(rest[:], ps[:, bank, :], part[:, 0, :], ALU.subtract)\
                        .then_inc(s_rest, 1)
                    dst = v_all[:, bass.ds(k, 1), :, :].rearrange("p a t (h w) -> p (a t h) w", w=VW)
                    nc.vector.tensor_copy(dst[:, :, 0:D], ps[:, bank + 1, 0:QT * C]
                                          .rearrange("p (h d) -> p h d", d=D)).then_inc(s_read, 1)
                elif kind == "turn_a":
                    nc.vector.tensor_copy(aT[0:C, :], ps[0:C, bank, :]).then_inc(s_read, 1)
                elif kind == "proj":
                    nc.vector.tensor_tensor(h1[:], by_tile(bank, C), hid[:, bass.ds(k * QT, QT), :], ALU.add)\
                        .then_inc(s_read, 1)
                elif kind == "ln2_sum":
                    dve.wait_ge(s_read, done - 1)
                    stand_alone(dve)
                    ln_sum(1, h1, k)
                elif kind == "ln2_var":
                    ln_var(1, k)
                elif kind == "turn_x2":
                    nc.vector.tensor_copy(x2T[0:C, :], ps[0:C, bank, :]).then_inc(s_read, 1)
                elif kind == "router":
                    nc.vector.tensor_copy(logits[:], by_tile(bank, E)).then_inc(s_read, 1)
                elif kind == "shift":
                    dve.wait_ge(s_read, done - 1)
                    step, _ = link(dve, s_route, k * ROUTE_STEPS)
                    stand_alone(dve)
                    step(nc.vector.tensor_reduce(top[:], logits[:], AX.X, ALU.max))
                    nc.vector.tensor_tensor(logits[:], logits[:], wide(top[:]), ALU.subtract).then_inc(s_route, 1)
                elif kind == "route":
                    route(k, item)
                elif kind == "turn_g":
                    nc.vector.tensor_copy(gT[:], ps[0:PARTS * E, bank, :]).then_inc(s_read, 1)
                elif kind in ("pick0", "pick1"):
                    a = int(kind[-1])
                    dve.wait_ge(s_gelu, k * 2 + a + 1)
                    nc.vector.tensor_tensor(gated[:, 2 * a:2 * a + 2, :], ps[:, bank:bank + 2, :],
                                            act_h[:, a, :, :], ALU.mult).then_inc(s_read, 1)
                elif kind == "down":
                    dve.wait_ge(s_free, (k + 1) * 16)
                    nc.vector.tensor_tensor(res[:], by_tile(bank, C), h1[:], ALU.add).then_inc(s_read, 1)
                    dve.wait_ge(s_read, done)
                    nc.vector.tensor_tensor(res[:], res[:], ln[1]["xn"][:], ALU.add).then_inc(s_res, 1)

            def run(p, i):
                for n in range(len(p.events)):
                    event(p, i, n)

            run_prologue(dve, run)
            run(HEAD, 0)
            run_bodies(dve, run)
            run(TAIL, BLOCKS)

        @block.scalar
        def _(act):
            act.wait_ge(s_kzero, 1)
            for j in range(HG):
                strip = k_slot[STRIP * j:STRIP * j + STRIP, :, j, :]
                nc.scalar.activation(strip, strip, ACT.Copy, bias=1.0).then_inc(s_kones, 1)

            def side(p, i, n):
                r, kind, unit, item = p.events[n]
                k = turn_of(p, i, kind)
                bank = 2 * ((p.at_ring + p.ring[n]) % 2)
                if kind == "numer":
                    act.wait_ge(s_route, k * ROUTE_STEPS + 2)
                    nc.scalar.activation(pr[:], logits[:], ACT.Exp).then_inc(s_pex, 1)
                elif kind in ("up0", "up1"):
                    act.wait_ge(s_fill, p.ring_at(i, n) + 1)
                    nc.scalar.activation(act_h[:, int(kind[-1]), :, :], ps[:, bank:bank + 2, :], ACT.Gelu)\
                        .then_inc(s_gelu, 1)

            def body(p, i):
                turned = {e[2]: n for n, e in enumerate(p.events) if e[1] == "turn_o"}
                for r in range(BODY + (O_EVAC + 1 if p.last else 0)):
                    for blk in (2 * r, 2 * r + 1) if r < BODY else ():
                        kc, j = blk // HG, blk % HG
                        act.wait_ge(s_score, i * SCORES + blk + 1)
                        if j == 0 and not (p.first and kc < PBUF):
                            act.wait_ge(s_pv, i * CHUNKS + kc - PBUF + 1)
                        nc.scalar.activation(prob[:, kc % PBUF, j, :], ps[:, SCORE + blk % SCORE_BANKS, :],
                                             ACT.Exp).then_inc(s_exp, 1)
                    if r % SLOTS == O_EVAC and not (p.first and r < SLOTS):
                        u = r // SLOTS - 1
                        act.wait_ge(s_pv, i * CHUNKS + TILES * (u + 1))
                        if u - 1 in turned:
                            act.wait_ge(s_fill, p.ring_at(i, turned[u - 1]) + 1)
                        elif u < 0:
                            since = BODY - ((UNITS - 1) * SLOTS + O_TURN)
                            act.wait_ge(s_fill, p.ring_at(i, 0) - since)
                        nc.scalar.activation(o_rows[:], ps[:, OBANK, :], ACT.Copy).then_inc(s_orow, 1)
                    for n, e in enumerate(p.events):
                        if e[0] == r:
                            side(p, i, n)

            run_bodies(act, body)
            for n in range(len(TAIL.events)):
                side(TAIL, BLOCKS, n)

        @block.tensor
        def _(pe):
            pe.wait_ge(s_w, 16 * 11)
            pe.wait_ge(s_const, 4 + 2 + 2 * PARTS)
            pe.wait_ge(s_b2, 5)
            pe.wait_ge(s_ones, 4)
            pe.wait_ge(s_opsum, 1)

            def tiles(bank, rows_, width=P):
                return [ps[0:rows_, bank, width * t:width * t + width] for t in range(QT)]

            def fill(p, i, n):
                r, kind, unit, item = p.events[n]
                k = turn_of(p, i, kind)
                bank = 2 * ((p.at_ring + p.ring[n]) % 2)

                if kind == "max":
                    q, j, h = item // 8, (item // 2) % HG, item % 2
                    u = unit % UNITS
                    if item == 0:
                        pe.wait_ge(s_qload[u], (i + unit // UNITS + 1) * (16 * HG))
                        pe.wait_ge(s_kload[u], (i + unit // UNITS + 1) * (16 * HG))
                    for c in range(2):
                        key = (2 * h + c) * 512
                        ins = nc.tensor.matmul(ps[:, bank + c, :], q_slot[:, u, P * q:P * q + P],
                                               k_slot[:, u, j, key:key + 512], start=True, stop=True)
                elif kind == "turn_m":
                    pe.wait_ge(s_mcols, i * UNITS + unit + 1)
                    for t, o in enumerate(tiles(bank, P)):
                        ins = nc.tensor.matmul(o, m_cols[:, t, :], ident16[:], start=True, stop=True)
                elif kind == "turn_o":
                    pe.wait_ge(s_orow, i * UNITS + unit + 1)
                    stand_alone(pe)
                    for t, o in enumerate(tiles(bank, P)):
                        ins = nc.tensor.transpose(o, o_rows[:, P * t:P * t + P], ident[:])
                elif kind in ("turn_x", "turn_a", "turn_x2"):
                    if kind == "turn_a":
                        src = attn
                    else:
                        w = int(kind == "turn_x2")
                        src = ln[w]["xn"]
                        pe.wait_ge(s_xn[w], k + 1)
                    stand_alone(pe)
                    for t, o in enumerate(tiles(bank, C)):
                        ins = nc.tensor.transpose(o, src[:, t, :], ident[:])
                elif kind == "qkv":
                    nc.tensor.matmul(ps[:, bank, :], wqkv[:, 0:2 * C], xT[:], start=True, stop=True)
                    for t, o in enumerate(tiles(bank + 1, P, C)):
                        ins = nc.tensor.matmul(o, xT[:, P * t:P * t + P], wqkv[:, 2 * C:3 * C],
                                               start=True, stop=True)
                elif kind == "proj":
                    for t, o in enumerate(tiles(bank, P, C)):
                        ins = nc.tensor.matmul(o, aT[:, P * t:P * t + P], wproj[:], start=True, stop=True)
                elif kind == "router":
                    for t, o in enumerate(tiles(bank, P, E)):
                        ins = nc.tensor.matmul(o, x2T[0:C, P * t:P * t + P], wroute[:], start=True, stop=True)
                elif kind == "turn_g":
                    pe.wait_ge(s_gcols, k + 1)
                    for t, o in enumerate(tiles(bank, PARTS * E)):
                        ins = nc.tensor.matmul(o, g_cols[:, t, :], ident16[:], start=True, stop=True)
                elif kind in ("up0", "up1"):
                    for c in range(2):
                        e = 2 * int(kind[-1]) + c
                        ins = nc.tensor.matmul(ps[:, bank + c, :], w1s[:, P * e:P * e + P], x2T[:],
                                               start=True, stop=True)
                elif kind in ("pick0", "pick1"):
                    for c in range(2):
                        ins = nc.tensor.matmul(ps[:, bank + c, :], pick[:, 2 * int(kind[-1]) + c, :], gT[:],
                                               start=True, stop=True)
                else:
                    for t, o in enumerate(tiles(bank, P, C)):
                        for e in range(E // 2):
                            nc.tensor.matmul(o, gated[:, e, P * t:P * t + P], w2s[:, e, :],
                                             start=(e == 0), stop=False)
                        for n_ in range(PARTS):
                            ins = nc.tensor.matmul(o, gT[:, P * t:P * t + P], b2p[:, n_, :],
                                                   start=False, stop=(n_ == PARTS - 1))
                return ins

            def event(p, i, n):
                if p.events[n][1] not in RING_KINDS:
                    return
                uses = [m for m in range(n) if p.events[m][1] in RING_KINDS]
                count = p.read_at(i, uses[-1]) if uses else p.read_at(i, n) - 1
                source = SOURCE.get(p.events[n][1])
                if source and source[0] == "turn_o" and p is TAIL:
                    count = p.at_read
                elif source:
                    m = p.find(*source)
                    if not uses or m >= uses[-1]:
                        count = p.read_at(i, m) + 1
                if above_zero(count):
                    pe.wait_ge(s_read, count)
                if len(uses) > 1 and p.events[uses[-2]][1] in ("up0", "up1"):
                    pe.wait_ge(s_gelu, turn_of(p, i, "up0") * 2 + int(p.events[uses[-2]][1][-1]) + 1)
                fill(p, i, n).then_inc(s_fill, 1)

            def run(p, i):
                for n in range(len(p.events)):
                    event(p, i, n)

            run_prologue(pe, run)
            pe.wait_ge(s_kones, HG)
            run(HEAD, 0)

            def scores(p, i, r):
                unit = r // SLOTS
                if r % SLOTS == 0:
                    if unit >= 1:
                        pe.wait_ge(s_read, p.read_at(i, p.find("turn_m", unit)) + 1)
                    elif p.first:
                        pe.wait_ge(s_read, HEAD.at_read + HEAD.reads)
                    else:
                        pe.wait_ge(s_read, p.read_at(i, 0) - (SLOTS - 1 - M_TURN))
                for blk in (2 * r, 2 * r + 1):
                    kc, j = blk // HG, blk % HG
                    if blk >= SCORE_BANKS:
                        pe.wait_ge(s_exp, i * SCORES + blk - SCORE_BANKS + 1)
                    elif not p.first:
                        left = next(m for m in range(SCORES) if (SCORES - 1 - m) % SCORE_BANKS == blk)
                        pe.wait_ge(s_exp, i * SCORES - left)
                    key = P * (kc % TILES)
                    nc.tensor.matmul(ps[:, SCORE + blk % SCORE_BANKS, :], k_slot[:, unit, j, key:key + P],
                                     q_full[:, unit % 2, :], start=True, stop=True).then_inc(s_score, 1)

            def values(p, i, k):
                unit, kc = k // TILES % UNITS, k % TILES
                pe.wait_ge(s_exp, i * SCORES + HG * (k + 1))
                if kc == 0:
                    if not (p.first and k == 0):
                        pe.wait_ge(s_orow, i * UNITS + unit)
                    pe.wait_ge(s_vload[unit], i + 1)
                for j in range(HG):
                    lo = STRIP * j
                    ins = nc.tensor.matmul(ps[lo:lo + VW, OBANK, :], v_slot[:, unit, kc, VW * j:VW * j + VW],
                                           prob[:, k % PBUF, j, :], start=(kc == 0), stop=(kc == TILES - 1),
                                           tile_position=(0, lo))
                ins.then_inc(s_pv, 1)

            def body(p, i):
                for r in range(BODY + (SLOTS if p.last else 0)):
                    here = [n for n, e in enumerate(p.events) if e[0] == r]
                    for n in here:
                        if p.events[n][1] == "max":
                            event(p, i, n)
                    if r < BODY:
                        scores(p, i, r)
                    for n in here:
                        if p.events[n][1] != "max":
                            event(p, i, n)
                    k = (r - PV_LAG) // 2
                    if (r - PV_LAG) % 2 == 0 and not (p.first and k < 0) and k < CHUNKS:
                        values(p, i, k)

            run_bodies(pe, body)
            run(TAIL, BLOCKS)


_INS = ["x", "itok_BS_0_99998", "L0_tok_weight", "L0_attn_w_qkv", "L0_attn_b_qkv", "L0_attn_w_proj",
        "L0_attn_b_proj", "L0_ffn_router_w", "L0_ffn_w1", "L0_ffn_b1", "L0_ffn_w2", "L0_ffn_b2"]


def kernel(**inputs):
    import numpy as np
    import concourse.bacc as bacc
    from concourse.bass_utils import run_bass_kernel_spmd

    nc = bacc.Bacc("TRN2", target_bir_lowering=False, num_devices=1)
    arrays, args = {}, []
    for name in _INS:
        a = np.ascontiguousarray(inputs[name])
        arrays[f"in_{name}"] = a
        args.append(nc.dram_tensor(f"in_{name}", a.shape, mybir.dt.from_np(a.dtype), kind="ExternalInput").ap())
    out = nc.dram_tensor("out", (B, N, C), F32, kind="ExternalOutput").ap()
    build(nc, *args, out)
    r = run_bass_kernel_spmd(nc, [arrays], core_ids=[0])
    return r.results[0]["out"]
```

```python
from contextlib import ExitStack

import concourse.bass as bass
from concourse import mybir
from concourse.alu_op_type import AluOpType as ALU

ACT = mybir.ActivationFunctionType
AX = mybir.AxisListType
F32 = mybir.dt.float32
BF16 = mybir.dt.bfloat16
I32 = mybir.dt.int32

P = 128
VOCAB, C = 25000, 64
B, N = 4, 2048
H, D = 16, 4
E = 8
EPS = 1e-5

TILES = N // P
QUARTERS = 4
QT = TILES // QUARTERS
BLK = QT * P
HALF = BLK // 2
BLOCKS = B * QUARTERS

GROUPS, HG = 4, 4
STRIP = 32
TERMS = [(0, 0), (0, 1), (0, 2), (1, 0), (1, 1), (2, 0)]
KROWS = D * len(TERMS)
PARTS = 3
STORES = 2 * len(TERMS)

UNITS = GROUPS
SLOTS = 32
BODY = UNITS * SLOTS
SCORES = 2 * BODY
CHUNKS = UNITS * TILES
LEAD = 7
PV_LAG = 5
PBUF = 4
VW = D + 1
SCORE_BANKS = 3

O_EVAC = 3
O_TURN = 9
V_COPY = 12
M_TURN = 29
EMBED, LN1_SUM, LN1_VAR, TURN_X, QK0, QK1, V, STORE, GATHER = 0, 3, 7, 13, 17, 21, 23, 24, 90
TURN_A, PROJ, LN2_SUM, LN2_VAR, TURN_X2, ROUTER, SHIFT, NUMER, ROUTE, SPLIT_G = 11, 15, 19, 25, 31, 35, 37, 39, 43, 62
UP, TURN_G, DOWN = 49, 67, 85
PICK = (69, 71, 75, 77)
ROUTES = 18

RING_KINDS = ("max", "turn_o", "turn_m", "turn_x", "qk0", "qk1", "v", "turn_a", "proj", "turn_x2", "router",
              "turn_g", "up0", "up1", "pick", "down")
PRO = [(EMBED, "embed"), (LN1_SUM, "ln1_sum"), (LN1_VAR, "ln1_var"), (TURN_X, "turn_x"), (QK0, "qk0"), (QK1, "qk1"),
       (V, "v"), (STORE, "store"), (GATHER, "gather")]
SOURCE = {"qk0": ("turn_x",), "qk1": ("turn_x",), "v": ("turn_x",), "turn_a": ("turn_o", -1), "proj": ("turn_a",),
          "router": ("turn_x2",), "pick": ("turn_g",), "down": ("pick", 0, E // 2 - 1)}
MOE = [(TURN_A, "turn_a"), (PROJ, "proj"), (LN2_SUM, "ln2_sum"), (LN2_VAR, "ln2_var"),
       (TURN_X2, "turn_x2"), (ROUTER, "router"), (SHIFT, "shift"), (NUMER, "numer"),
       *((ROUTE + n, "route", n) for n in range(UP - ROUTE)), (UP, "up0"), (UP, "up1"),
       *((ROUTE + n, "route", n) for n in range(UP - ROUTE, ROUTES)), (SPLIT_G, "split_g"),
       (TURN_G, "turn_g"), *((PICK[n], "pick", n) for n in range(E // 2)), (DOWN, "down")]


def events_of(first, last, pro, moe):
    out = []
    for r in range(BODY + (SLOTS if last else 0)):
        ahead = r + SLOTS + LEAD
        if not (last and ahead >= BODY):
            out.append((r, "max", ahead // SLOTS, ahead % SLOTS))
        u = r // SLOTS
        if r % SLOTS == O_TURN and not (first and u == 0) and u <= UNITS:
            out.append((r, "turn_o", u - 1, 0))
        if r % SLOTS == M_TURN and not (last and u + 1 >= UNITS):
            out.append((r, "turn_m", u + 1, 0))
        out += [(r, kind, 0, *(step or [0])) for at, kind, *step in PRO if pro and at == r]
        out += [(r, kind, 0, *(step or [0])) for at, kind, *step in MOE if moe and at == r]
    return out


class Part:

    def __init__(self, start, stop, events, at_ring, at_read, first=False, last=False):
        self.start, self.stop, self.events, self.first, self.last = start, stop, events, first, last
        self.at_ring, self.at_read = at_ring, at_read
        self.ring, self.read = [], []
        ring = read = 0
        for e in events:
            self.ring.append(ring)
            self.read.append(read)
            if e[1] in RING_KINDS:
                ring += 1
                read += e[1] not in ("up0", "up1")
        self.rings, self.reads = ring, read

    def ring_at(self, i, n):
        return self.counted(i, self.rings, self.at_ring + self.ring[n])

    def read_at(self, i, n):
        return self.counted(i, self.reads, self.at_read + self.read[n])

    def counted(self, i, each, at):
        return i * each + (at - self.start * each) if self.start != self.stop else at

    def find(self, kind, unit=0, item=0):
        for n, e in enumerate(self.events):
            if e[1:] == (kind, unit, item):
                return n
        raise KeyError((kind, unit, item))

    def after(self):
        turns = max(self.stop - self.start, 1)
        return self.at_ring + turns * self.rings, self.at_read + turns * self.reads


def plan():
    parts, at = [], (0, 0)

    def add(start, stop, events, **kw):
        nonlocal at
        parts.append(Part(start, stop, events, *at, **kw))
        at = parts[-1].after()

    add(0, QUARTERS, [(0, kind, 0, *(step or [0])) for _, kind, *step in PRO])
    head = [(n, "max", n // SLOTS, n % SLOTS) for n in range(SLOTS + LEAD)] + [(SLOTS + LEAD, "turn_m", 0, 0)]
    add(0, 0, head)
    add(0, 0, events_of(True, False, True, False), first=True)
    with_pro = BLOCKS - QUARTERS
    add(1, with_pro, events_of(False, False, True, True))
    add(with_pro, BLOCKS - 1, events_of(False, False, False, True))
    add(BLOCKS - 1, BLOCKS - 1, events_of(False, True, False, True), last=True)
    add(BLOCKS, BLOCKS, [(0, kind, 0, *(step or [0])) for _, kind, *step in MOE])
    for p in parts:
        assert p.stop - p.start <= 1 or p.rings % 2 == 0
    return parts


PROLOGUE, HEAD, *BODIES, TAIL = plan()


def run_bodies(eng, emit):
    for part in BODIES:
        if part.stop == part.start:
            emit(part, part.start)
        else:
            with eng.Fori(part.start, part.stop) as i:
                emit(part, i)


def run_prologue(eng, emit):
    emit(PROLOGUE, 0)
    with eng.Fori(1, QUARTERS) as x:
        emit(PROLOGUE, x)


def above_zero(value):
    return not isinstance(value, int) or value > 0


def build(nc, x, itok, table, w_qkv, b_qkv, w_proj, b_proj, router_w, w1, b1, w2, b2, out):
    with ExitStack() as ctx:
        def sb(name, shape, dt=F32):
            return ctx.enter_context(nc.sbuf_tensor(name, shape, dt))

        def sem(name):
            return ctx.enter_context(nc.semaphore(name))

        q_rows = nc.dram_tensor("q_rows", (BLOCKS, GROUPS, P, BLK), BF16, kind="Internal").ap()
        k_rows = nc.dram_tensor("k_rows", (B, GROUPS, P, N), BF16, kind="Internal").ap()

        ps = ctx.enter_context(nc.psum_tensor("ps", [P, 8, 512], F32))
        SCORE, OBANK = 4, 7

        ident = sb("ident", [P, P])
        ident16 = sb("ident16", [P, P], BF16)
        wqkv = sb("wqkv", [C + 1, 3 * C])
        wproj = sb("wproj", [C + 1, C])
        wroute = sb("wroute", [C, E])
        w1s = sb("w1s", [C + 1, E * C])
        w2s = sb("w2s", [P, E // 2, C])
        b2s = sb("b2s", [PARTS * E, C])
        b2r = sb("b2r", [PARTS * E, C])
        b2p = sb("b2p", [PARTS * E, PARTS, C], BF16)
        pick = sb("pick", [PARTS * E, E // 2, P], BF16)
        fillers = sb("fillers", [P, 2], BF16)
        minus_half = sb("minus_half", [P, QT])
        order = sb("order", [P, E])

        ids = sb("ids", [P, 2, B * TILES], I32)
        idsf = sb("idsf", [P, 2, B * TILES])
        negf = sb("negf", [P, 2, B * TILES])
        rows = sb("rows", [P, 2, B * TILES + QT], I32)
        differ_i = sb("differ_i", [P, B * TILES], I32)
        differ = sb("differ", [P, B * TILES])
        hid = sb("hid", [P, B * TILES, C])
        v_all = sb("v_all", [P, BLOCKS, QT, H * VW])

        row_now = sb("row_now", [P, 2, QT], I32)
        emb = sb("emb", [P, 2, QT, C])
        ln = [{k: sb(f"ln{n}_{k}", [P, QT] if k in ("sum", "var", "y", "t") else [P, QT, C])
               for k in ("sum", "var", "y", "t", "xc", "sq", "xn")} for n in (1, 2)]
        xT = sb("xT", [C + 1, BLK])
        part = sb("part", [P, PARTS, BLK], BF16)
        rest = sb("rest", [P, BLK])

        k_slot = sb("k_slot", [P, GROUPS, HG, N], BF16)
        q_slot = sb("q_slot", [P, UNITS, BLK], BF16)
        v_slot = sb("v_slot", [P, GROUPS, TILES, HG * VW])
        q_full = sb("q_full", [P, 2, BLK], BF16)
        prob = sb("prob", [P, PBUF, HG, BLK])
        half_max = sb("half_max", [P, 2, 2, QT * HG])
        neg_max = sb("neg_max", [P, QT, HG])
        rest_max = sb("rest_max", [P, QT, HG])
        m_cols = sb("m_cols", [P, QT, P], BF16)
        o_rows = sb("o_rows", [P, BLK])
        recip = sb("recip", [P, QT, HG])
        attn = sb("attn", [P, QT, C])

        aT = sb("aT", [C + 1, BLK])
        h1 = sb("h1", [P, QT, C])
        x2T = sb("x2T", [C + 1, BLK])
        logits = sb("logits", [P, QT, E])
        top = sb("top", [P, QT])
        pr = sb("pr", [P, QT, E])
        gate = sb("gate", [P, QT, E])
        hot = sb("hot", [P, QT, E])
        g_rest = sb("g_rest", [P, QT, E])
        g_cols = sb("g_cols", [P, QT, PARTS * E], BF16)
        gT = sb("gT", [PARTS * E, BLK], BF16)
        act_h = sb("act_h", [P, 2, 2, BLK])
        gated = sb("gated", [P, E // 2, BLK])
        res = sb("res", [P, QT, C])

        s_passed = sem("waits_passed")
        s_zeroed = sem("pool_zeroed")
        s_const = sem("constants_ready")
        s_w = sem("weights_loaded")
        s_b2 = sem("b2_steps")
        s_ones = sem("token_ones_ready")
        s_fillers = sem("fillers_ready")
        s_kzero = sem("key_slots_zero")
        s_kones = sem("key_strips_one")
        s_opsum = sem("output_bank_zeroed")
        s_ids = sem("ids_loaded")
        s_idstep = sem("id_steps")
        s_row = sem("rows_ready")
        s_rownow = sem("row_now_ready")
        s_gather = sem("gathered")
        s_mask = sem("second_masked")
        s_emb = sem("embedded")
        s_sum = [sem(f"ln{n}_sum_ready") for n in (1, 2)]
        s_sq = [sem(f"ln{n}_squares_ready") for n in (1, 2)]
        s_var = [sem(f"ln{n}_var_steps") for n in (1, 2)]
        s_lnp = [sem(f"ln{n}_pool_steps") for n in (1, 2)]
        s_xn = [sem(f"ln{n}_ready") for n in (1, 2)]
        s_hi = sem("hi_ready")
        s_mid = sem("mid_ready")
        s_lo = sem("lo_ready")
        s_mid_first = sem("mid_ready_first_batch")
        s_lo_first = sem("lo_ready_first_batch")
        s_store = sem("rows_stored")
        s_kload = [sem(f"k_loaded_{n}") for n in range(GROUPS)]
        s_qload = [sem(f"q_loaded_{n}") for n in range(UNITS)]
        s_vload = [sem(f"v_copied_{n}") for n in range(GROUPS)]
        s_fill = sem("ring_filled")
        s_read = sem("ring_read")
        s_neg = sem("neg_max_ready")
        s_pmax = sem("max_steps")
        s_mcols = sem("m_cols_ready")
        s_score = sem("scores_filled")
        s_exp = sem("exps_done")
        s_pv = sem("pv_done")
        s_orow = sem("o_rows_ready")
        s_rec = sem("recip_ready")
        s_shift = sem("logits_shifted")
        s_route = sem("route_steps")
        s_pex = sem("numerators_ready")
        s_gstep = sem("gate_steps")
        s_gcols = sem("gate_cols_ready")
        s_gelu = sem("gelu_ready")
        s_res = sem("result_ready")
        s_free = sem("result_buffer_free")

        block = ctx.enter_context(nc.Block())

        def flat(ap):
            return ap.rearrange("p a b -> p (a b)")

        def stand_alone(eng):
            eng.sem_inc(s_passed, 1)

        def link(eng, s, base):
            n = [0]

            def step(ins):
                n[0] += 1
                ins.then_inc(s, 1)
                eng.wait_ge(s, base + n[0])
            return step, n

        def turn_of(p, i, kind):
            if kind in [e[1] for e in MOE]:
                return i - 1
            return i if p is PROLOGUE else i + QUARTERS

        LNP_STEPS, VAR_STEPS, ROUTE_STEPS, MAX_STEPS = 7, 1, 2 + ROUTES, 3

        @block.sync
        def _(sp):
            for n, src in enumerate((x, itok)):
                sp.dma_start(ids[:, n, :].rearrange("p (b t) -> p b t", b=B),
                             src.rearrange("b (p t) -> p b t", p=P)).then_inc(s_ids, 16)
            loads = [
                (wqkv[0:C, :], w_qkv),
                (wqkv[C:C + 1, :], b_qkv.rearrange("(a n) -> a n", a=1)),
                (wproj[0:C, :], w_proj),
                (wproj[C:C + 1, :], b_proj.rearrange("(a n) -> a n", a=1)),
                (w1s[0:C, :].rearrange("i (e o) -> i e o", e=E), w1.rearrange("e i o -> i e o")),
                (w1s[C:C + 1, :], b1.rearrange("(a e) o -> a (e o)", a=1)),
                (w2s[:], w2.rearrange("(r e) i o -> (e i) r o", e=2)),
            ] + [(b2s[E * n:E * n + E, :], b2) for n in range(PARTS)]
            for dst, src in loads:
                sp.dma_start(dst, src).then_inc(s_w, 16)
            sp.dma_start(wroute[:], router_w.rearrange("e c -> c e"),
                         allow_slow_non_contiguous=True).then_inc(s_w, 16)
            sp.sem_inc(s_free, 16)

            def store_rows(xb):
                for t, (pq, pk) in enumerate(TERMS):
                    qd = q_rows[bass.ds(xb, 1), :, :, :]
                    kd = k_rows[bass.ds(xb // QUARTERS, 1), :, :, bass.ds(xb % QUARTERS * BLK, BLK)]
                    for dst, side, p0 in ((qd, pq, 0), (kd, pk, C)):
                        d = dst.rearrange("a g (j r) n -> (a g) j r n", r=STRIP)[:, :, D * t:D * t + D, :]
                        sp.dma_start(d, part[p0:p0 + C, side, :]).then_inc(s_store, 16)

            def load_k(g, i):
                for j in range(HG):
                    lo = STRIP * j
                    sp.dma_start(k_slot[lo:lo + KROWS, g, j, :],
                                 k_rows[bass.ds(i // QUARTERS, 1), g, lo:lo + KROWS, :]
                                 .rearrange("a r n -> (a r) n")).then_inc(s_kload[g], 16)

            def load_q(u, i):
                for j in range(HG):
                    lo = STRIP * j
                    sp.dma_start(q_slot[lo:lo + KROWS, u, :],
                                 q_rows[bass.ds(i, 1), u, lo:lo + KROWS, :].rearrange("a r n -> (a r) n"))\
                        .then_inc(s_qload[u], 16)

            def prologue(p, xb):
                sp.wait_ge(s_lo_first, xb + 1)
                store_rows(xb)
            run_prologue(sp, prologue)
            sp.wait_ge(s_store, 16 * STORES * QUARTERS)
            sp.wait_ge(s_kones, HG)
            sp.wait_ge(s_const, 4)
            for u in range(UNITS):
                load_q(u, 0)
                load_k(u, 0)

            def body(p, i):
                if any(e[1] == "store" for e in p.events):
                    sp.wait_ge(s_lo, i + 1)
                    store_rows(i + QUARTERS)
                    sp.wait_ge(s_store, (i + QUARTERS + 1) * (16 * STORES))
                for u in range(UNITS if not p.last else 0):
                    sp.wait_ge(s_exp, i * SCORES + (u + 1) * 2 * SLOTS)
                    load_q(u, i + 1)
                    load_k(u, i + 1)
                    if u == 1 and not p.first:
                        store_out(i - 1)
                if p.last:
                    store_out(i - 1)

            def store_out(m):
                sp.wait_ge(s_res, m + 1)
                dst = out[bass.ds(m // QUARTERS, 1), :, :].rearrange("a (p q t) c -> (a p) q (t c)", p=P, q=QUARTERS)
                sp.dma_start(dst[:, bass.ds(m % QUARTERS, 1), :],
                             res[:].rearrange("p t c -> p (t c)").unsqueeze(1)).then_inc(s_free, 16)

            run_bodies(sp, body)
            store_out(BLOCKS - 1)
            sp.wait_ge(s_free, 16 * (BLOCKS + 1))

        @block.gpsimd
        def _(pool):
            for n in range(2):
                nc.gpsimd.memset(fillers[:, n:n + 1], float(n)).then_inc(s_fillers, 1)
            nc.gpsimd.memset(ident[:], 0.0).then_inc(s_zeroed, 1)
            nc.gpsimd.memset(ident16[:], 0.0).then_inc(s_zeroed, 1)
            nc.gpsimd.memset(pick[:], 0.0).then_inc(s_zeroed, 1)
            nc.gpsimd.memset(q_slot[:], 0.0).then_inc(s_const, 1)
            nc.gpsimd.memset(m_cols[:], 0.0).then_inc(s_const, 1)
            nc.gpsimd.memset(minus_half[:], -0.5).then_inc(s_const, 1)
            nc.gpsimd.iota(order[:], [[-1, E]], base=E, channel_multiplier=0,
                           allow_small_or_imprecise_dtypes=True).then_inc(s_const, 1)

            def take_rows(xb):
                nc.gpsimd.tensor_copy(row_now[:], rows[:, :, bass.ds(xb * QT, QT)]).then_inc(s_rownow, 1)
                pool.wait_ge(s_rownow, xb + 1)
                stand_alone(pool)

            def gather(start, stop):
                for m in range(start, stop):
                    t, n = m // 2, m % 2
                    nc.gpsimd.indirect_dma_start(
                        out=emb[:, n, t, :], out_offset=None, in_=table,
                        in_offset=bass.IndirectOffsetOnAxis(ap=row_now[:, n, t:t + 1], axis=0))\
                        .then_inc(s_gather, 16)

            def embed(xb):
                pool.wait_ge(s_gather, (xb + 1) * (2 * QT * 16))
                mask = differ[:, bass.ds(xb * QT, QT)].unsqueeze(2).to_broadcast([P, QT, C])
                nc.gpsimd.tensor_tensor(emb[:, 1, :, :], emb[:, 1, :, :], mask, ALU.mult).then_inc(s_mask, 1)
                pool.wait_ge(s_mask, xb + 1)
                stand_alone(pool)
                nc.gpsimd.tensor_tensor(hid[:, bass.ds(xb * QT, QT), :], emb[:, 0, :, :], emb[:, 1, :, :], ALU.add)\
                    .then_inc(s_emb, 1)

            def wide(a):
                return a.unsqueeze(2).to_broadcast([P, QT, C])

            def ln_squares(w, src, k):
                step, _ = link(pool, s_lnp[w], k * LNP_STEPS)
                pool.wait_ge(s_sum[w], k + 1)
                stand_alone(pool)
                step(nc.gpsimd.tensor_scalar(ln[w]["t"][:], ln[w]["sum"][:], -1.0 / C, 0.0, ALU.mult, ALU.add))
                stand_alone(pool)
                step(nc.gpsimd.tensor_tensor(ln[w]["xc"][:], src, wide(ln[w]["t"][:]), ALU.add))
                nc.gpsimd.tensor_tensor(ln[w]["sq"][:], ln[w]["xc"][:], ln[w]["xc"][:], ALU.mult)\
                    .then_inc(s_sq[w], 1)

            def ln_scale(w, k):
                step, n = link(pool, s_lnp[w], k * LNP_STEPS + 2)
                pool.wait_ge(s_var[w], (k + 1) * (VAR_STEPS + 1))
                t, y, v = (ln[w][a] for a in ("t", "y", "var"))
                step(nc.gpsimd.tensor_tensor(y[:], v[:], minus_half[:], ALU.pow))
                step(nc.gpsimd.tensor_tensor(t[:], y[:], y[:], ALU.mult))
                step(nc.gpsimd.tensor_tensor(t[:], t[:], v[:], ALU.mult))
                stand_alone(pool)
                step(nc.gpsimd.tensor_scalar(t[:], t[:], -0.5, 1.5, ALU.mult, ALU.add))
                step(nc.gpsimd.tensor_tensor(y[:], y[:], t[:], ALU.mult))
                nc.gpsimd.tensor_tensor(ln[w]["xn"][:], ln[w]["xc"][:], wide(y[:]), ALU.mult).then_inc(s_xn[w], 1)
                assert n[0] + 2 == LNP_STEPS

            def split_qk(xb, read):
                pool.wait_ge(s_read, read)
                stand_alone(pool)
                nc.gpsimd.tensor_copy(part[:, 1, :], rest[:]).then_inc(s_mid, 1)
                pool.wait_ge(s_mid, xb - QUARTERS + 1)
                nc.gpsimd.tensor_tensor(part[:, 2, :], rest[:], part[:, 1, :], ALU.subtract).then_inc(s_lo, 1)

            def copy_v(g, i):
                src = v_all[:, bass.ds(i // QUARTERS * QUARTERS, QUARTERS), :, g * HG * VW:(g + 1) * HG * VW]
                stand_alone(pool)
                nc.gpsimd.tensor_copy(v_slot[:, g, :, :].rearrange("p (q t) v -> p q t v", q=QUARTERS), src)\
                    .then_inc(s_vload[g], 1)

            def split_max(index, turned):
                step, _ = link(pool, s_pmax, index * MAX_STEPS)
                pool.wait_ge(s_neg, index + 1)
                if above_zero(turned):
                    pool.wait_ge(s_fill, turned)
                cols = m_cols[:].rearrange("p q (j r) -> p q j r", r=STRIP)
                stand_alone(pool)
                step(nc.gpsimd.tensor_copy(cols[:, :, :, KROWS], neg_max[:]))
                step(nc.gpsimd.tensor_tensor(rest_max[:], neg_max[:], cols[:, :, :, KROWS], ALU.subtract))
                stand_alone(pool)
                step(nc.gpsimd.tensor_copy(cols[:, :, :, KROWS + 1], rest_max[:]))
                nc.gpsimd.tensor_tensor(cols[:, :, :, KROWS + 2], rest_max[:], cols[:, :, :, KROWS + 1],
                                        ALU.subtract).then_inc(s_mcols, 1)

            def split_gates(m):
                step, _ = link(pool, s_gstep, m * MAX_STEPS)
                pool.wait_ge(s_route, (m + 1) * ROUTE_STEPS)
                stand_alone(pool)
                step(nc.gpsimd.tensor_copy(g_cols[:, :, 0:E], gate[:]))
                step(nc.gpsimd.tensor_tensor(g_rest[:], gate[:], g_cols[:, :, 0:E], ALU.subtract))
                stand_alone(pool)
                step(nc.gpsimd.tensor_copy(g_cols[:, :, E:2 * E], g_rest[:]))
                nc.gpsimd.tensor_tensor(g_cols[:, :, 2 * E:3 * E], g_rest[:], g_cols[:, :, E:2 * E],
                                        ALU.subtract).then_inc(s_gcols, 1)

            def side(p, i, kind):
                k = turn_of(p, i, kind)
                if kind == "embed":
                    embed(k)
                elif kind == "ln1_sum":
                    ln_squares(0, hid[:, bass.ds(k * QT, QT), :], k)
                elif kind == "ln1_var":
                    ln_scale(0, k)
                elif kind == "qk1":
                    split_qk(k, p.read_at(i, p.find("qk1")) + 1)
                elif kind == "ln2_sum":
                    ln_squares(1, h1[:], k)
                elif kind == "ln2_var":
                    ln_scale(1, k)
                elif kind == "split_g":
                    split_gates(k)

            pool.wait_ge(s_row, 1)
            take_rows(0)
            gather(0, 2 * QT)
            pool.wait_ge(s_zeroed, 2)
            for m in (ident, ident16):
                nc.gpsimd.affine_select(out=m[:], in_=m[:], compare_op=ALU.not_equal, fill=1.0, base=0,
                                        pattern=[[-1, P]], channel_multiplier=1).then_inc(s_const, 1)
            def prologue(p, xb):
                embed(xb)
                take_rows(xb + 1)
                gather(0, 3)
                side(p, xb, "ln1_sum")
                gather(3, 5)
                side(p, xb, "ln1_var")
                gather(5, 2 * QT)
            run_prologue(pool, prologue)

            pool.wait_ge(s_read, HEAD.at_read)
            for g in range(GROUPS):
                copy_v(g, 0)
            split_max(0, 0)
            pool.wait_ge(s_zeroed, 3)
            for n in range(PARTS):
                for e in range(2):
                    half = pick[:, :, C * e:C * e + C]
                    nc.gpsimd.affine_select(out=half, in_=half, compare_op=ALU.not_equal, fill=1.0,
                                            base=-(E * n + e), pattern=[[-2, E // 2], [0, C]],
                                            channel_multiplier=1).then_inc(s_const, 1)
                    pool.wait_ge(s_const, 6 + 2 * n + e + 1)
            pool.wait_ge(s_w, 16 * 11)
            step, _ = link(pool, s_b2, 0)
            step(nc.gpsimd.memset(b2p[:], 0.0))
            step(nc.gpsimd.tensor_copy(b2p[:, 0, :], b2s[:]))
            step(nc.gpsimd.tensor_tensor(b2r[:], b2s[:], b2p[:, 0, :], ALU.subtract))
            step(nc.gpsimd.tensor_copy(b2p[:, 1, :], b2r[:]))
            step(nc.gpsimd.tensor_tensor(b2p[:, 2, :], b2r[:], b2p[:, 1, :], ALU.subtract))


            def body(p, i):
                n_turn = {e[2]: n for n, e in enumerate(p.events) if e[1] == "turn_m"}
                for n, (r, kind, unit, item) in enumerate(p.events):
                    if kind == "max" and item == SLOTS - 1:
                        if unit - 1 in n_turn:
                            turned = p.ring_at(i, n_turn[unit - 1]) + 1
                        elif p.first:
                            turned = HEAD.at_ring + HEAD.rings
                        else:
                            left = BODY - (SLOTS * (UNITS - 1) + M_TURN) - 1
                            turned = p.ring_at(i, 0) - left
                        split_max(i * UNITS + unit, turned)
                    if kind == "gather":
                        take_rows(i + QUARTERS + 1)
                        gather(0, 2 * QT)
                    side(p, i, kind)
                    if kind == "max" and r % SLOTS == V_COPY:
                        g = r // SLOTS - 1
                        if g >= 0 and not p.last and g < UNITS - 1:
                            pool.wait_ge(s_pv, i * CHUNKS + (g + 1) * TILES)
                            copy_v(g, i + 1)
                        if g == -1 and not p.first:
                            pool.wait_ge(s_pv, i * CHUNKS)
                            copy_v(UNITS - 1, i)

            run_bodies(pool, body)
            for _, kind, _, _ in TAIL.events:
                side(TAIL, BLOCKS, kind)
            pool.wait_ge(s_gather, (BLOCKS + 1) * 2 * QT * 16)

        @block.vector
        def _(dve):
            dve.wait_ge(s_ids, 32)
            step, _ = link(dve, s_idstep, 0)
            step(nc.vector.tensor_copy(idsf[:], ids[:]))
            step(nc.vector.tensor_scalar(negf[:], idsf[:], 0.0, float(VOCAB), ALU.is_lt, ALU.mult))
            step(nc.vector.tensor_tensor(idsf[:], idsf[:], negf[:], ALU.add))
            step(nc.vector.tensor_scalar(idsf[:], idsf[:], 0.0, float(VOCAB - 1), ALU.max, ALU.min))
            step(nc.vector.memset(rows[:], 0))
            step(nc.vector.tensor_copy(rows[:, :, 0:B * TILES], idsf[:]))
            step(nc.vector.tensor_tensor(differ_i[:], ids[:, 0, :], ids[:, 1, :], ALU.bitwise_xor))
            nc.vector.tensor_scalar(differ[:], differ_i[:], 0.0, None, ALU.not_equal).then_inc(s_row, 1)
            for t in (xT, aT, x2T):
                nc.vector.memset(t[:], 1.0).then_inc(s_ones, 1)
            nc.vector.memset(v_all[:], 1.0).then_inc(s_ones, 1)
            nc.vector.memset(ps[:, OBANK, :], 0.0).then_inc(s_opsum, 1)
            dve.wait_ge(s_ones, 4)

            def ln_sum(w, src, k):
                nc.vector.reduce_sum(ln[w]["sum"][:], src, AX.X).then_inc(s_sum[w], 1)

            def ln_var(w, k):
                step, _ = link(dve, s_var[w], k * (VAR_STEPS + 1))
                dve.wait_ge(s_sq[w], k + 1)
                step(nc.vector.reduce_sum(ln[w]["var"][:], ln[w]["sq"][:], AX.X))
                nc.vector.tensor_scalar(ln[w]["var"][:], ln[w]["var"][:], 1.0 / C, EPS, ALU.mult, ALU.add)\
                    .then_inc(s_var[w], 1)

            def wide(a):
                return a.unsqueeze(2).to_broadcast([P, QT, E])

            def route(m, n):
                lg, g = logits[:], gate[:]
                by_order = order[:].unsqueeze(1).to_broadcast([P, QT, E])
                if n == 0:
                    dve.wait_ge(s_pex, m + 1)
                else:
                    dve.wait_ge(s_route, m * ROUTE_STEPS + 2 + n)
                if n == 0:
                    ins = nc.vector.reduce_sum(top[:], pr[:], AX.X)
                elif n == 1:
                    ins = nc.vector.reciprocal(top[:], top[:])
                elif n == 2:
                    ins = nc.vector.tensor_tensor(pr[:], pr[:], wide(top[:]), ALU.mult)
                elif n == 3:
                    ins = nc.vector.scalar_tensor_tensor(hot[:], lg, 0.0, by_order, ALU.is_equal, ALU.mult)
                elif n == 4:
                    ins = nc.vector.tensor_reduce(top[:], hot[:], AX.X, ALU.max)
                elif n == 5:
                    ins = nc.vector.tensor_tensor(g, by_order, wide(top[:]), ALU.is_equal)
                elif n == 6:
                    ins = nc.vector.scalar_tensor_tensor(lg, g, -3.0e38, lg, ALU.mult, ALU.add)
                elif n == 7:
                    ins = nc.vector.tensor_reduce(top[:], lg, AX.X, ALU.max)
                elif n == 8:
                    ins = nc.vector.tensor_tensor(hot[:], lg, wide(top[:]), ALU.is_equal)
                elif n == 9:
                    ins = nc.vector.tensor_tensor(hot[:], hot[:], by_order, ALU.mult)
                elif n == 10:
                    ins = nc.vector.tensor_reduce(top[:], hot[:], AX.X, ALU.max)
                elif n == 11:
                    ins = nc.vector.tensor_tensor(hot[:], by_order, wide(top[:]), ALU.is_equal)
                elif n == 12:
                    ins = nc.vector.tensor_tensor(g, g, hot[:], ALU.add)
                elif n == 13:
                    ins = nc.vector.tensor_tensor(g, g, pr[:], ALU.mult)
                elif n == 14:
                    ins = nc.vector.reduce_sum(top[:], g, AX.X)
                elif n == 15:
                    ins = nc.vector.tensor_scalar(top[:], top[:], 1e-12, None, ALU.max)
                elif n == 16:
                    ins = nc.vector.reciprocal(top[:], top[:])
                else:
                    ins = nc.vector.tensor_tensor(g, g, wide(top[:]), ALU.mult)
                ins.then_inc(s_route, 1)

            def by_tile(bank, width):
                return ps[:, bank, 0:QT * width].rearrange("p (t c) -> p t c", c=width)

            def join(index, parity, done):
                dve.wait_ge(s_read, done)
                if above_zero(index):
                    dve.wait_ge(s_mcols, index)
                halves = half_max[:, parity, :, :]
                nc.vector.tensor_tensor(flat(neg_max[:]), halves[:, 0, :], halves[:, 1, :], ALU.min)\
                    .then_inc(s_neg, 1)

            def event(p, i, n):
                r, kind, unit, item = p.events[n]
                k = turn_of(p, i, kind)
                use = p.at_ring + p.ring[n]
                bank = 2 * (use % 2)
                done = p.read_at(i, n) + 1
                if kind in RING_KINDS and kind not in ("up0", "up1"):
                    dve.wait_ge(s_fill, p.ring_at(i, n) + 1)
                if kind == "max":
                    q, j, h = item // 8, (item // 2) % HG, item % 2
                    nc.vector.tensor_reduce(half_max[:, unit % 2, h, HG * q + j:HG * q + j + 1],
                                            ps[:, bank:bank + 2, :], AX.XY, ALU.max, negate=True).then_inc(s_read, 1)
                    if item == 0 and p is not HEAD:
                        join(i * UNITS + unit - 1, (unit - 1) % 2, done - 1)
                    elif item == 0 and unit == 1:
                        join(0, 0, done - 1)
                    elif item == SLOTS - 1 and p.last and unit == UNITS - 1:
                        join(i * UNITS + unit, unit % 2, done)
                elif kind == "turn_m":
                    if not (p is HEAD or p.first and unit < 2):
                        dve.wait_ge(s_exp, i * SCORES + (unit - 1) * 2 * SLOTS)
                    nc.vector.tensor_tensor(q_full[:, unit % 2, :], ps[:, bank, :], q_slot[:, unit % UNITS, :],
                                            ALU.add).then_inc(s_read, 1)
                elif kind == "turn_o":
                    ot = ps[:, bank, :].rearrange("p (q j r) -> p q j r", q=QT, r=STRIP)
                    dve.wait_ge(s_read, done - 1)
                    nc.vector.reciprocal(recip[:], ot[:, :, :, D]).then_inc(s_rec, 1)
                    dve.wait_ge(s_rec, i * UNITS + unit + 1)
                    g = unit % UNITS
                    dst = attn[:, :, g * HG * D:(g + 1) * HG * D].rearrange("p q (j d) -> p q j d", d=D)
                    nc.vector.tensor_tensor(dst, ot[:, :, :, 0:D],
                                            recip[:].unsqueeze(3).to_broadcast([P, QT, HG, D]),
                                            ALU.mult).then_inc(s_read, 1)
                elif kind == "ln1_sum":
                    dve.wait_ge(s_emb, k + 1)
                    stand_alone(dve)
                    ln_sum(0, hid[:, bass.ds(k * QT, QT), :], k)
                elif kind == "ln1_var":
                    ln_var(0, k)
                elif kind == "turn_x":
                    nc.vector.tensor_copy(xT[0:C, :], ps[0:C, bank, :]).then_inc(s_read, 1)
                elif kind in ("qk0", "qk1"):
                    h = int(kind[-1])
                    cols = slice(h * HALF, (h + 1) * HALF)
                    if h == 0 and above_zero(k):
                        dve.wait_ge(s_store, k * (16 * STORES))
                    nc.vector.tensor_copy(part[:, 0, cols], ps[:, bank, 0:HALF]).then_inc(s_hi, 1)
                    dve.wait_ge(s_hi, k * 2 + h + 1)
                    nc.vector.tensor_tensor(rest[:, cols], ps[:, bank, 0:HALF], part[:, 0, cols], ALU.subtract)\
                        .then_inc(s_read, 1)
                    if p is PROLOGUE and h == 1:
                        dve.wait_ge(s_read, done)
                        nc.vector.tensor_copy(part[:, 1, :], rest[:]).then_inc(s_mid_first, 1)
                        dve.wait_ge(s_mid_first, k + 1)
                        nc.vector.tensor_tensor(part[:, 2, :], rest[:], part[:, 1, :], ALU.subtract)\
                            .then_inc(s_lo_first, 1)
                elif kind == "v":
                    dst = v_all[:, bass.ds(k, 1), :, :].rearrange("p a t (h w) -> p (a t h) w", w=VW)
                    nc.vector.tensor_copy(dst[:, :, 0:D], ps[:, bank, 0:QT * C]
                                          .rearrange("p (h d) -> p h d", d=D)).then_inc(s_read, 1)
                elif kind == "turn_a":
                    nc.vector.tensor_copy(aT[0:C, :], ps[0:C, bank, :]).then_inc(s_read, 1)
                elif kind == "proj":
                    nc.vector.tensor_tensor(h1[:], by_tile(bank, C), hid[:, bass.ds(k * QT, QT), :], ALU.add)\
                        .then_inc(s_read, 1)
                elif kind == "ln2_sum":
                    dve.wait_ge(s_read, done - 1)
                    stand_alone(dve)
                    ln_sum(1, h1[:], k)
                elif kind == "ln2_var":
                    ln_var(1, k)
                elif kind == "turn_x2":
                    nc.vector.tensor_copy(x2T[0:C, :], ps[0:C, bank, :]).then_inc(s_read, 1)
                elif kind == "router":
                    nc.vector.tensor_copy(logits[:], by_tile(bank, E)).then_inc(s_read, 1)
                elif kind == "shift":
                    dve.wait_ge(s_read, done - 1)
                    step, _ = link(dve, s_route, k * ROUTE_STEPS)
                    stand_alone(dve)
                    step(nc.vector.tensor_reduce(top[:], logits[:], AX.X, ALU.max))
                    nc.vector.tensor_tensor(logits[:], logits[:], wide(top[:]), ALU.subtract).then_inc(s_route, 1)
                elif kind == "route":
                    route(k, item)
                elif kind == "turn_g":
                    nc.vector.tensor_copy(gT[:], ps[0:PARTS * E, bank, :]).then_inc(s_read, 1)
                elif kind == "pick":
                    if item % 2 == 0:
                        dve.wait_ge(s_gelu, k * 2 + item // 2 + 1)
                    nc.vector.tensor_tensor(gated[:, item, :], ps[:, bank, :], act_h[:, item // 2, item % 2, :],
                                            ALU.mult).then_inc(s_read, 1)
                elif kind == "down":
                    dve.wait_ge(s_free, (k + 1) * 16)
                    nc.vector.tensor_tensor(res[:], by_tile(bank, C), h1[:], ALU.add).then_inc(s_read, 1)
                    dve.wait_ge(s_read, done)
                    nc.vector.tensor_tensor(res[:], res[:], ln[1]["xn"][:], ALU.add).then_inc(s_res, 1)

            def run(p, i):
                for n in range(len(p.events)):
                    event(p, i, n)

            run_prologue(dve, run)
            run(HEAD, 0)
            run_bodies(dve, run)
            run(TAIL, BLOCKS)

        @block.scalar
        def _(act):
            act.wait_ge(s_fillers, 2)
            for g in range(GROUPS):
                nc.scalar.activation(k_slot[:, g, :, :].rearrange("p j n -> p (j n)"),
                                     fillers[:, 0:1].to_broadcast([P, HG * N]), ACT.Copy).then_inc(s_kzero, 1)
            act.wait_ge(s_kzero, GROUPS)
            for j in range(HG):
                strip = k_slot[STRIP * j:STRIP * j + STRIP, :, j, :]
                nc.scalar.activation(strip, fillers[STRIP * j:STRIP * j + STRIP, 1:2].unsqueeze(1)
                                     .to_broadcast([STRIP, GROUPS, N]), ACT.Copy).then_inc(s_kones, 1)

            def side(p, i, n):
                r, kind, unit, item = p.events[n]
                k = turn_of(p, i, kind)
                bank = 2 * ((p.at_ring + p.ring[n]) % 2)
                if kind == "numer":
                    act.wait_ge(s_route, k * ROUTE_STEPS + 2)
                    nc.scalar.activation(pr[:], logits[:], ACT.Exp).then_inc(s_pex, 1)
                elif kind in ("up0", "up1"):
                    act.wait_ge(s_fill, p.ring_at(i, n) + 1)
                    nc.scalar.activation(act_h[:, int(kind[-1]), :, :], ps[:, bank:bank + 2, :], ACT.Gelu)\
                        .then_inc(s_gelu, 1)

            def body(p, i):
                turned = {e[2]: n for n, e in enumerate(p.events) if e[1] == "turn_o"}
                for r in range(BODY + (O_EVAC + 1 if p.last else 0)):
                    for blk in (2 * r, 2 * r + 1) if r < BODY else ():
                        kc, j = blk // HG, blk % HG
                        act.wait_ge(s_score, i * SCORES + blk + 1)
                        if j == 0 and not (p.first and kc < PBUF):
                            act.wait_ge(s_pv, i * CHUNKS + kc - PBUF + 1)
                        nc.scalar.activation(prob[:, kc % PBUF, j, :], ps[:, SCORE + blk % SCORE_BANKS, :],
                                             ACT.Exp).then_inc(s_exp, 1)
                    if r % SLOTS == O_EVAC and not (p.first and r < SLOTS):
                        u = r // SLOTS - 1
                        act.wait_ge(s_pv, i * CHUNKS + TILES * (u + 1))
                        if u - 1 in turned:
                            act.wait_ge(s_fill, p.ring_at(i, turned[u - 1]) + 1)
                        elif u < 0:
                            since = BODY - ((UNITS - 1) * SLOTS + O_TURN)
                            act.wait_ge(s_fill, p.ring_at(i, 0) - since)
                        nc.scalar.activation(o_rows[:], ps[:, OBANK, :], ACT.Copy).then_inc(s_orow, 1)
                    for n, e in enumerate(p.events):
                        if e[0] == r:
                            side(p, i, n)

            run_bodies(act, body)
            for n in range(len(TAIL.events)):
                side(TAIL, BLOCKS, n)

        @block.tensor
        def _(pe):
            pe.wait_ge(s_w, 16 * 11)
            pe.wait_ge(s_const, 4 + 2)
            pe.wait_ge(s_ones, 4)
            pe.wait_ge(s_opsum, 1)

            def tiles(bank, rows_, width=P):
                return [ps[0:rows_, bank, width * t:width * t + width] for t in range(QT)]

            def fill(p, i, n):
                r, kind, unit, item = p.events[n]
                k = turn_of(p, i, kind)
                bank = 2 * ((p.at_ring + p.ring[n]) % 2)

                if kind == "max":
                    q, j, h = item // 8, (item // 2) % HG, item % 2
                    u = unit % UNITS
                    if item == 0:
                        pe.wait_ge(s_qload[u], (i + unit // UNITS + 1) * (16 * HG))
                        pe.wait_ge(s_kload[u], (i + unit // UNITS + 1) * (16 * HG))
                    for c in range(2):
                        key = (2 * h + c) * 512
                        ins = nc.tensor.matmul(ps[:, bank + c, :], q_slot[:, u, P * q:P * q + P],
                                               k_slot[:, u, j, key:key + 512], start=True, stop=True)
                elif kind == "turn_m":
                    pe.wait_ge(s_mcols, i * UNITS + unit + 1)
                    for t, o in enumerate(tiles(bank, P)):
                        ins = nc.tensor.matmul(o, m_cols[:, t, :], ident16[:], start=True, stop=True)
                elif kind == "turn_o":
                    pe.wait_ge(s_orow, i * UNITS + unit + 1)
                    stand_alone(pe)
                    for t, o in enumerate(tiles(bank, P)):
                        ins = nc.tensor.transpose(o, o_rows[:, P * t:P * t + P], ident[:])
                elif kind in ("turn_x", "turn_a", "turn_x2"):
                    if kind == "turn_a":
                        src = attn
                    else:
                        w = int(kind == "turn_x2")
                        src = ln[w]["xn"]
                        pe.wait_ge(s_xn[w], k + 1)
                    stand_alone(pe)
                    for t, o in enumerate(tiles(bank, C)):
                        ins = nc.tensor.transpose(o, src[:, t, :], ident[:])
                elif kind in ("qk0", "qk1"):
                    h = int(kind[-1])
                    ins = nc.tensor.matmul(ps[:, bank, 0:HALF], wqkv[:, 0:2 * C], xT[:, h * HALF:(h + 1) * HALF],
                                           start=True, stop=True)
                elif kind == "v":
                    for t, o in enumerate(tiles(bank, P, C)):
                        ins = nc.tensor.matmul(o, xT[:, P * t:P * t + P], wqkv[:, 2 * C:3 * C],
                                               start=True, stop=True)
                elif kind == "proj":
                    for t, o in enumerate(tiles(bank, P, C)):
                        ins = nc.tensor.matmul(o, aT[:, P * t:P * t + P], wproj[:], start=True, stop=True)
                elif kind == "router":
                    for t, o in enumerate(tiles(bank, P, E)):
                        ins = nc.tensor.matmul(o, x2T[0:C, P * t:P * t + P], wroute[:], start=True, stop=True)
                elif kind == "turn_g":
                    pe.wait_ge(s_gcols, k + 1)
                    for t, o in enumerate(tiles(bank, PARTS * E)):
                        ins = nc.tensor.matmul(o, g_cols[:, t, :], ident16[:], start=True, stop=True)
                elif kind in ("up0", "up1"):
                    for c in range(2):
                        e = 2 * int(kind[-1]) + c
                        ins = nc.tensor.matmul(ps[:, bank + c, :], w1s[:, P * e:P * e + P], x2T[:],
                                               start=True, stop=True)
                elif kind == "pick":
                    ins = nc.tensor.matmul(ps[:, bank, :], pick[:, item, :], gT[:], start=True, stop=True)
                else:
                    for t, o in enumerate(tiles(bank, P, C)):
                        for e in range(E // 2):
                            nc.tensor.matmul(o, gated[:, e, P * t:P * t + P], w2s[:, e, :],
                                             start=(e == 0), stop=False)
                        for n_ in range(PARTS):
                            ins = nc.tensor.matmul(o, gT[:, P * t:P * t + P], b2p[:, n_, :],
                                                   start=False, stop=(n_ == PARTS - 1))
                return ins

            def event(p, i, n):
                if p.events[n][1] not in RING_KINDS:
                    return
                uses = [m for m in range(n) if p.events[m][1] in RING_KINDS]
                count = p.read_at(i, uses[-1]) if uses else p.read_at(i, n) - 1
                source = SOURCE.get(p.events[n][1])
                if source and source[0] == "turn_o" and p is TAIL:
                    count = p.at_read
                elif source:
                    m = p.find(*source)
                    if not uses or m >= uses[-1]:
                        count = p.read_at(i, m) + 1
                if above_zero(count):
                    pe.wait_ge(s_read, count)
                if len(uses) > 1 and p.events[uses[-2]][1] in ("up0", "up1"):
                    pe.wait_ge(s_gelu, turn_of(p, i, "up0") * 2 + int(p.events[uses[-2]][1][-1]) + 1)
                fill(p, i, n).then_inc(s_fill, 1)

            def run(p, i):
                for n in range(len(p.events)):
                    event(p, i, n)

            run_prologue(pe, run)
            pe.wait_ge(s_kones, HG)
            run(HEAD, 0)
            pe.wait_ge(s_const, 4 + 2 + 2 * PARTS)
            pe.wait_ge(s_b2, 5)

            def scores(p, i, r, blks):
                unit = r // SLOTS
                if r % SLOTS == 0:
                    if unit >= 1:
                        pe.wait_ge(s_read, p.read_at(i, p.find("turn_m", unit)) + 1)
                    elif p.first:
                        pe.wait_ge(s_read, HEAD.at_read + HEAD.reads)
                    else:
                        pe.wait_ge(s_read, p.read_at(i, 0) - (SLOTS - 1 - M_TURN))
                for blk in blks:
                    kc, j = blk // HG, blk % HG
                    if blk >= SCORE_BANKS:
                        pe.wait_ge(s_exp, i * SCORES + blk - SCORE_BANKS + 1)
                    elif not p.first:
                        left = next(m for m in range(SCORES) if (SCORES - 1 - m) % SCORE_BANKS == blk)
                        pe.wait_ge(s_exp, i * SCORES - left)
                    key = P * (kc % TILES)
                    nc.tensor.matmul(ps[:, SCORE + blk % SCORE_BANKS, :], k_slot[:, unit, j, key:key + P],
                                     q_full[:, unit % 2, :], start=True, stop=True).then_inc(s_score, 1)

            def values(p, i, k):
                unit, kc = k // TILES % UNITS, k % TILES
                pe.wait_ge(s_exp, i * SCORES + HG * (k + 1))
                if kc == 0:
                    if not (p.first and k == 0):
                        pe.wait_ge(s_orow, i * UNITS + unit)
                    pe.wait_ge(s_vload[unit], i + 1)
                for j in range(HG):
                    lo = STRIP * j
                    ins = nc.tensor.matmul(ps[lo:lo + VW, OBANK, :], v_slot[:, unit, kc, VW * j:VW * j + VW],
                                           prob[:, k % PBUF, j, :], start=(kc == 0), stop=(kc == TILES - 1),
                                           tile_position=(0, lo))
                ins.then_inc(s_pv, 1)

            def body(p, i):
                for r in range(BODY + (SLOTS if p.last else 0)):
                    here = [n for n, e in enumerate(p.events) if e[0] == r]
                    blks = (2 * r, 2 * r + 1) if r < BODY else ()
                    if r % 2 == 0:
                        if blks:
                            scores(p, i, r, blks)
                        for n in here:
                            event(p, i, n)
                        continue
                    first = [n for n in here if p.events[n][1] == "max"]
                    for n in first:
                        event(p, i, n)
                    if blks:
                        scores(p, i, r, blks[:1])
                    k = (r - PV_LAG) // 2
                    if not (p.first and k < 0) and k < CHUNKS:
                        values(p, i, k)
                    if blks:
                        scores(p, i, r, blks[1:])
                    for n in here[len(first):]:
                        event(p, i, n)

            run_bodies(pe, body)
            run(TAIL, BLOCKS)


_INS = ["x", "itok_BS_0_99998", "L0_tok_weight", "L0_attn_w_qkv", "L0_attn_b_qkv", "L0_attn_w_proj",
        "L0_attn_b_proj", "L0_ffn_router_w", "L0_ffn_w1", "L0_ffn_b1", "L0_ffn_w2", "L0_ffn_b2"]


def kernel(**inputs):
    import numpy as np
    import concourse.bacc as bacc
    from concourse.bass_utils import run_bass_kernel_spmd

    nc = bacc.Bacc("TRN2", target_bir_lowering=False, num_devices=1)
    arrays, args = {}, []
    for name in _INS:
        a = np.ascontiguousarray(inputs[name])
        arrays[f"in_{name}"] = a
        args.append(nc.dram_tensor(f"in_{name}", a.shape, mybir.dt.from_np(a.dtype), kind="ExternalInput").ap())
    out = nc.dram_tensor("out", (B, N, C), F32, kind="ExternalOutput").ap()
    build(nc, *args, out)
    r = run_bass_kernel_spmd(nc, [arrays], core_ids=[0])
    return r.results[0]["out"]
```
